# Optimizing a Trainium2 kernel written in Bass

```python
import numpy as np
import jax
import jax.numpy as jnp

def _softmax(x, axis=-1):
    return jax.nn.softmax(x, axis=axis)

def _gelu(x):
    return jax.nn.gelu(x, approximate=True)

def _silu(x):
    return jax.nn.silu(x)

def _sigmoid(x):
    return jax.nn.sigmoid(x)

def _layernorm(x, axis=-1, eps=1e-05):
    m = jnp.mean(x, axis=axis, keepdims=True)
    v = jnp.var(x, axis=axis, keepdims=True)
    return (x - m) / jnp.sqrt(v + eps)

def _scatter_add(tgt, idx, src, axis=0):
    return tgt.at[idx].add(src)

def _segment_sum(src, seg, n):
    return jax.ops.segment_sum(src, seg, n)
kernel_name = 'mk_cond_resid_d4_seqx_r2_d6897f'

def setup_inputs(seed: int=0):
    np.random.seed(seed)
    _w = jnp.asarray

    def _rec_inputs():
        import jax
        import jax.numpy as jnp
        _rk = jax.random.key(seed)
        x = -0.000125 + 0.9999 * jax.random.normal(jax.random.fold_in(_rk, 1), (32, 128, 2048), jnp.float32)
        _lenS = 128 - jax.random.randint(jax.random.fold_in(_rk, 7), (32,), 0, max(1, 128 // 4) + 1, jnp.int32)
        _lenS2 = 128 - jax.random.randint(jax.random.fold_in(_rk, 8), (32,), 0, max(1, 128 // 4) + 1, jnp.int32)
        cond_128 = 0.0061147 + 1.02565 * jax.random.normal(jax.random.fold_in(_rk, 11), (32, 128), jnp.float32)
        fside_S_0 = -0.022604 + 0.987366 * jax.random.normal(jax.random.fold_in(_rk, 12), (128,), jnp.float32)
        return (x, cond_128, fside_S_0)
    x, cond_128, fside_S_0 = _rec_inputs()

    def _L0_cond_setup():
        import jax, jax.numpy as jnp
        import numpy as np
        from jax import lax
        N, C_IN, L = (32, 128, 2048)
        C_OUT, K, GROUPS = (128, 9, 4)
        C_DIM, PAD, STRIDE = (128, 4, 1)
        key = jax.random.key(seed)
        k1, k2, k3, k4, k5 = jax.random.split(key, 5)
        x = jax.random.normal(k1, (N, C_IN, L), dtype=jnp.float32)
        c = jax.random.normal(k2, (N, C_DIM), dtype=jnp.float32)
        weight = jax.random.normal(k3, (C_OUT, C_IN // GROUPS, K), dtype=jnp.float32)
        c_weight = jax.random.normal(k4, (C_OUT, C_DIM), dtype=jnp.float32)
        bias = jax.random.normal(k5, (C_OUT,), dtype=jnp.float32)
        return {'x': x, 'c': c, 'weight': weight, 'c_weight': c_weight, 'bias': bias}
    _L0_cond_all = _L0_cond_setup()
    _L0_cond_in = {k: v for k, v in _L0_cond_all.items() if k in ('weight', 'c_weight')}
    del _L0_cond_all

    def _L1_cond_setup():
        import jax, jax.numpy as jnp
        import numpy as np
        K = 8
        T = 1.0
        D_EMBD = 128
        IN_C = 128
        OUT_C = 128
        BS = 32
        H = 2048
        HID = 128
        key = jax.random.key(seed)
        ks = jax.random.split(key, 10)
        s = lambda fan_in: 1.0 / np.sqrt(fan_in)
        return {'x': jax.random.normal(ks[0], (BS, IN_C, H), dtype=jnp.float32), 'embedding': jax.random.normal(ks[1], (BS, D_EMBD), dtype=jnp.float32), 'W0': jax.random.normal(ks[2], (D_EMBD, HID), dtype=jnp.float32) * s(D_EMBD), 'b0': jnp.zeros((HID,), dtype=jnp.float32), 'W1': jax.random.normal(ks[3], (HID, HID), dtype=jnp.float32) * s(HID), 'b1': jnp.zeros((HID,), dtype=jnp.float32), 'W2': jax.random.normal(ks[4], (HID, K), dtype=jnp.float32) * s(HID), 'b2': jnp.zeros((K,), dtype=jnp.float32), 'weight': jax.random.normal(ks[5], (K, OUT_C, IN_C, 1), dtype=jnp.float32) * s(IN_C), 'bias_k': jax.random.normal(ks[6], (K, OUT_C), dtype=jnp.float32) * 0.1}
    _L1_cond_all = _L1_cond_setup()
    _L1_cond_in = {k: v for k, v in _L1_cond_all.items() if k in ('W0', 'b0', 'W1', 'b1', 'W2', 'b2', 'weight', 'bias_k')}
    del _L1_cond_all

    def _L2_cond_setup():
        import jax, jax.numpy as jnp
        import numpy as np
        from jax import lax
        N, C_IN, L = (32, 128, 2048)
        C_OUT, K, GROUPS = (128, 9, 4)
        C_DIM, PAD, STRIDE = (128, 4, 1)
        key = jax.random.key(seed)
        k1, k2, k3, k4, k5 = jax.random.split(key, 5)
        x = jax.random.normal(k1, (N, C_IN, L), dtype=jnp.float32)
        c = jax.random.normal(k2, (N, C_DIM), dtype=jnp.float32)
        weight = jax.random.normal(k3, (C_OUT, C_IN // GROUPS, K), dtype=jnp.float32)
        c_weight = jax.random.normal(k4, (C_OUT, C_DIM), dtype=jnp.float32)
        bias = jax.random.normal(k5, (C_OUT,), dtype=jnp.float32)
        return {'x': x, 'c': c, 'weight': weight, 'c_weight': c_weight, 'bias': bias}
    _L2_cond_all = _L2_cond_setup()
    _L2_cond_in = {k: v for k, v in _L2_cond_all.items() if k in ('weight', 'c_weight')}
    del _L2_cond_all

    def _L3_cond_setup():
        import jax, jax.numpy as jnp
        import numpy as np
        K = 8
        T = 1.0
        D_EMBD = 128
        IN_C = 128
        OUT_C = 128
        BS = 32
        H = 2048
        HID = 128
        key = jax.random.key(seed)
        ks = jax.random.split(key, 10)
        s = lambda fan_in: 1.0 / np.sqrt(fan_in)
        return {'x': jax.random.normal(ks[0], (BS, IN_C, H), dtype=jnp.float32), 'embedding': jax.random.normal(ks[1], (BS, D_EMBD), dtype=jnp.float32), 'W0': jax.random.normal(ks[2], (D_EMBD, HID), dtype=jnp.float32) * s(D_EMBD), 'b0': jnp.zeros((HID,), dtype=jnp.float32), 'W1': jax.random.normal(ks[3], (HID, HID), dtype=jnp.float32) * s(HID), 'b1': jnp.zeros((HID,), dtype=jnp.float32), 'W2': jax.random.normal(ks[4], (HID, K), dtype=jnp.float32) * s(HID), 'b2': jnp.zeros((K,), dtype=jnp.float32), 'weight': jax.random.normal(ks[5], (K, OUT_C, IN_C, 1), dtype=jnp.float32) * s(IN_C), 'bias_k': jax.random.normal(ks[6], (K, OUT_C), dtype=jnp.float32) * 0.1}
    _L3_cond_all = _L3_cond_setup()
    _L3_cond_in = {k: v for k, v in _L3_cond_all.items() if k in ('W0', 'b0', 'W1', 'b1', 'W2', 'b2', 'weight', 'bias_k')}
    del _L3_cond_all
    return {'x': x, 'cond_128': cond_128, 'fside_S_0': fside_S_0, 'L0_cond_weight': _L0_cond_in['weight'], 'L0_cond_c_weight': _L0_cond_in['c_weight'], 'L1_cond_W0': _L1_cond_in['W0'], 'L1_cond_b0': _L1_cond_in['b0'], 'L1_cond_W1': _L1_cond_in['W1'], 'L1_cond_b1': _L1_cond_in['b1'], 'L1_cond_W2': _L1_cond_in['W2'], 'L1_cond_b2': _L1_cond_in['b2'], 'L1_cond_weight': _L1_cond_in['weight'], 'L1_cond_bias_k': _L1_cond_in['bias_k'], 'L2_cond_weight': _L2_cond_in['weight'], 'L2_cond_c_weight': _L2_cond_in['c_weight'], 'L3_cond_W0': _L3_cond_in['W0'], 'L3_cond_b0': _L3_cond_in['b0'], 'L3_cond_W1': _L3_cond_in['W1'], 'L3_cond_b1': _L3_cond_in['b1'], 'L3_cond_W2': _L3_cond_in['W2'], 'L3_cond_b2': _L3_cond_in['b2'], 'L3_cond_weight': _L3_cond_in['weight'], 'L3_cond_bias_k': _L3_cond_in['bias_k']}

def reference(x, cond_128, fside_S_0, L0_cond_weight, L0_cond_c_weight, L1_cond_W0, L1_cond_b0, L1_cond_W1, L1_cond_b1, L1_cond_W2, L1_cond_b2, L1_cond_weight, L1_cond_bias_k, L2_cond_weight, L2_cond_c_weight, L3_cond_W0, L3_cond_b0, L3_cond_W1, L3_cond_b1, L3_cond_W2, L3_cond_b2, L3_cond_weight, L3_cond_bias_k):
    import jax
    import jax.numpy as jnp

    def _L0_cond_ref(x, c, weight, c_weight, bias):
        import jax, jax.numpy as jnp
        import numpy as np
        from jax import lax
        N, C_IN, L = (32, 128, 2048)
        C_OUT, K, GROUPS = (128, 9, 4)
        C_DIM, PAD, STRIDE = (128, 4, 1)
        out = lax.conv_general_dilated(x, weight, window_strides=(STRIDE,), padding=[(PAD, PAD)], dimension_numbers=('NCH', 'OIH', 'NCH'), feature_group_count=GROUPS)
        ctx = jnp.einsum('nd,od->no', c, c_weight)
        out = out + ctx[:, :, None] + bias[None, :, None]
        return out

    def _L1_cond_ref(x, embedding, W0, b0, W1, b1, W2, b2, weight, bias_k):
        import jax, jax.numpy as jnp
        import numpy as np
        K = 8
        T = 1.0
        D_EMBD = 128
        IN_C = 128
        OUT_C = 128
        BS = 32
        H = 2048
        HID = 128
        h = jax.nn.gelu(embedding @ W0 + b0, approximate=False)
        h = jax.nn.gelu(h @ W1 + b1, approximate=False)
        att = jax.nn.softmax((h @ W2 + b2) / T, axis=-1)
        agg_w = jnp.einsum('bk,koi->boi', att, weight[..., 0])
        agg_b = att @ bias_k
        out = jnp.einsum('boi,bih->boh', agg_w, x) + agg_b[:, :, None]
        return out

    def _L2_cond_ref(x, c, weight, c_weight, bias):
        import jax, jax.numpy as jnp
        import numpy as np
        from jax import lax
        N, C_IN, L = (32, 128, 2048)
        C_OUT, K, GROUPS = (128, 9, 4)
        C_DIM, PAD, STRIDE = (128, 4, 1)
        out = lax.conv_general_dilated(x, weight, window_strides=(STRIDE,), padding=[(PAD, PAD)], dimension_numbers=('NCH', 'OIH', 'NCH'), feature_group_count=GROUPS)
        ctx = jnp.einsum('nd,od->no', c, c_weight)
        out = out + ctx[:, :, None] + bias[None, :, None]
        return out

    def _L3_cond_ref(x, embedding, W0, b0, W1, b1, W2, b2, weight, bias_k):
        import jax, jax.numpy as jnp
        import numpy as np
        K = 8
        T = 1.0
        D_EMBD = 128
        IN_C = 128
        OUT_C = 128
        BS = 32
        H = 2048
        HID = 128
        h = jax.nn.gelu(embedding @ W0 + b0, approximate=False)
        h = jax.nn.gelu(h @ W1 + b1, approximate=False)
        att = jax.nn.softmax((h @ W2 + b2) / T, axis=-1)
        agg_w = jnp.einsum('bk,koi->boi', att, weight[..., 0])
        agg_b = att @ bias_k
        out = jnp.einsum('boi,bih->boh', agg_w, x) + agg_b[:, :, None]
        return out
    x = x + _L0_cond_ref(x, cond_128, L0_cond_weight, L0_cond_c_weight, fside_S_0)
    x = x + _L1_cond_ref(x, cond_128, L1_cond_W0, L1_cond_b0, L1_cond_W1, L1_cond_b1, L1_cond_W2, L1_cond_b2, L1_cond_weight, L1_cond_bias_k)
    x = x + _L2_cond_ref(x, cond_128, L2_cond_weight, L2_cond_c_weight, fside_S_0)
    x = x + _L3_cond_ref(x, cond_128, L3_cond_W0, L3_cond_b0, L3_cond_W1, L3_cond_b1, L3_cond_W2, L3_cond_b2, L3_cond_weight, L3_cond_bias_k)
    return x

_drawn_inputs = setup_inputs


def setup_inputs(seed=0):
    import zlib

    import numpy as np

    out = dict(_drawn_inputs(seed))
    spreads = {'L1_cond_b0': (0.0, 0.626),
     'L1_cond_b1': (0.0, 0.441),
     'L1_cond_b2': (0.0, 0.343),
     'L3_cond_b0': (0.0, 0.551),
     'L3_cond_b1': (0.0, 0.358),
     'L3_cond_b2': (0.0, 0.283)}
    factors = {'L1_cond_bias_k': 35.962, 'L3_cond_bias_k': 64.0}
    for name, (base, spread) in spreads.items():
        noise = np.random.default_rng([zlib.crc32(name.encode()), seed]).standard_normal(out[name].shape)
        drawn = base * np.exp(spread * noise) if base else spread * noise
        out[name] = jnp.asarray(drawn.astype(out[name].dtype))
    for name, factor in factors.items():
        out[name] = (out[name] * factor).astype(out[name].dtype)
    return out
```

```python
from contextlib import ExitStack

import concourse.bass as bass
from concourse import mybir

F32 = mybir.dt.float32
ALU = mybir.AluOpType
ACT = mybir.ActivationFunctionType
AX = mybir.AxisListType

P = 128
NB = 32
L = 2048
G = 4
CG = P // G
K = 9
PH = P // CG
N = L // PH
NE = 8
REACH = 3
NS = 2
PAIRS = NB // NS
MOVES = PH * G


def build(nc, t, out):
    ctx = ExitStack()
    with ctx:
        def sb(name, shape, dt=F32):
            return ctx.enter_context(nc.sbuf_tensor(name, shape, dt))

        def sem(name):
            return ctx.enter_context(nc.semaphore(name))

        cond_t = sb("cond_t", [P, NB])
        eye = sb("eye_sb", [P, P])
        fside = sb("fside_sb", [P, 1])
        toep = [sb(f"toep{l}", [P, G, PH, REACH, CG]) for l in range(2)]
        cw_t = [sb(f"cw_t{l}", [P, P]) for l in range(2)]
        w0 = [sb(f"w0_{l}", [P, P]) for l in range(2)]
        w1 = [sb(f"w1_{l}", [P, P]) for l in range(2)]
        w2 = [sb(f"w2_{l}", [P, NE]) for l in range(2)]
        b0 = [sb(f"b0_{l}", [P, 1]) for l in range(2)]
        b1 = [sb(f"b1_{l}", [P, 1]) for l in range(2)]
        b2 = [sb(f"b2_{l}", [NB, NE]) for l in range(2)]
        experts = [sb(f"experts{l}", [P, NE, P]) for l in range(2)]
        bias_k = [sb(f"bias_k{l}", [NE, P]) for l in range(2)]
        hid = [sb(f"hid{l}", [P, 2, NB]) for l in range(2)]
        logit = [sb(f"logit{l}", [NB, NE]) for l in range(2)]
        top = [sb(f"top{l}", [NB, 1]) for l in range(2)]
        expo = [sb(f"expo{l}", [NB, NE]) for l in range(2)]
        total = [sb(f"total{l}", [NB, 1]) for l in range(2)]
        att = [sb(f"att{l}", [NB, NE]) for l in range(2)]
        att_diag = [sb(f"att_diag{l}", [NB, NB, NE]) for l in range(2)]
        att_t = [sb(f"att_t{l}", [NE, NB]) for l in range(2)]
        ones = sb("ones", [NB, P])
        att_all = [sb(f"att_all{l}", [P, NB, NE]) for l in range(2)]
        biases = sb("biases", [P, NB, 3 + G])
        bias_now = [sb(f"bias_now{s}", [P, 3 + G]) for s in range(NS)]
        x_in = [sb(f"x_in{s}", [P, L]) for s in range(NS)]
        x_ph = [sb(f"x_ph{s}", [P, PH, N]) for s in range(NS)]
        conv_in = [[sb(f"conv_in{l}_{s}", [P, G, N + 2]) for s in range(NS)] for l in range(2)]
        mix_in = [[sb(f"mix_in{l}_{s}", [P, PH, N]) for s in range(NS)] for l in range(2)]
        y_out = [sb(f"y_out{s}", [P, L]) for s in range(NS)]
        prod = [sb(f"prod{l}", [P, NE, P]) for l in range(2)]
        mat = [[sb(f"mat{l}_{s}", [P, P]) for s in range(NS)] for l in range(2)]
        banks = [ctx.enter_context(nc.psum_tensor(f"bank{i}", [P, N], F32)) for i in range(8)]

        loads = []
        loads.append((cond_t, t["cond_t"]))
        for l in range(2):
            loads += [(w0[l], t[f"w0_{l}"]), (b0[l], t[f"b0_{l}"]), (w1[l], t[f"w1_{l}"]),
                      (b1[l], t[f"b1_{l}"]), (w2[l], t[f"w2_{l}"]), (b2[l], t[f"b2_{l}"]),
                      (bias_k[l], t[f"bias_k{l}"]), (cw_t[l], t[f"cw_t{l}"])]
        loads += [(eye, t["eye"]), (fside, t["fside"])]
        for l in range(2):
            loads += [(toep[l], t[f"toep{l}"]), (experts[l], t[f"experts{l}"])]
        ALL = 16 * len(loads)

        consts = sem("consts")
        x_loaded = [sem(f"x_loaded{s}") for s in range(NS)]
        x_split = sem("x_split")
        x_moved = [sem(f"x_moved{s}") for s in range(NS)]
        conv_done = [sem(f"conv_done{l}") for l in range(2)]
        mix_done = [sem(f"mix_done{l}") for l in range(2)]
        mix_in_ready = [sem(f"mix_in_ready{l}") for l in range(2)]
        conv1_in_ready = sem("conv1_in_ready")
        y_ready = sem("y_ready")
        y_stored = [sem(f"y_stored{s}") for s in range(NS)]
        mat_ready = [sem(f"mat_ready{l}") for l in range(2)]
        pool_step = sem("pool_step")
        dve_step = sem("dve_step")
        act_step = sem("act_step")
        s_z = sem("mlp_product")
        s_h = sem("hidden_ready")
        s_att = sem("att_stage")
        s_pe = sem("setup_product")
        setup_dve = sem("setup_dve")
        bias_ready = sem("bias_ready")

        def sample(i, s):
            return i * NS + s

        def bias(s, col):
            return bias_now[s][:, col:col + 1]

        def each_pair(eng, body):
            with eng.Fori(0, PAIRS - 1) as i:
                body(i, False)
            body(PAIRS - 1, True)

        block = ctx.enter_context(nc.Block())

        @block.sync
        def _(sp):
            def load_x(b, s):
                sp.dma_start(x_in[s][:], t["x"][bass.ds(b, 1), :, :].rearrange("b c l -> (b c) l")
                             ).then_inc(x_loaded[s], 16)

            def move_x(i, s):
                sp.wait_ge(x_split, sample(i, s) + 1)
                for p in range(PH):
                    for g in range(G):
                        sp.dma_start(conv_in[0][s][CG * p:CG * (p + 1), g, 1:N + 1],
                                     x_ph[s][CG * g:CG * (g + 1), p, :]).then_inc(x_moved[s], 16)

            for s in range(NS):
                load_x(s, s)
            for dst, src in loads:
                sp.dma_start(dst[:], src).then_inc(consts, 16)
            sp.wait_ge(setup_dve, 1)
            for s in range(NS):
                move_x(0, s)
            for s in range(NS):
                sp.wait_ge(x_split, s + 1)
                load_x(NS + s, s)

            def pair(i, last):
                if not last:
                    for s in range(NS):
                        move_x(i + 1, s)
                for s in range(NS):
                    b = sample(i, s)
                    sp.wait_ge(y_ready, PH * (b + 1))
                    sp.dma_start(out[bass.ds(b, 1), :, :].rearrange("b c l -> (b c) l"), y_out[s][:]
                                 ).then_inc(y_stored[s], 16)

            def body(i, last):
                pair(i, last)

            with sp.Fori(0, PAIRS - 2) as i:
                pair(i, False)
                for s in range(NS):
                    sp.wait_ge(x_split, sample(i + 1, s) + 1)
                    load_x(sample(i + 2, s), s)
            pair(PAIRS - 2, False)
            pair(PAIRS - 1, True)
            for s in range(NS):
                sp.wait_ge(y_stored[s], 16 * PAIRS)

        @block.gpsimd
        def _(pool):
            nc.gpsimd.memset(ones[:], 1.0).then_inc(pool_step, 1)
            pool.wait_ge(s_att, 6)
            pool.wait_ge(consts, ALL)
            STEPS = 4

            def mix_matrix(l, i, s, first):
                b = sample(i, s)
                done = (b * 2 + l) * STEPS + 1
                if not first:
                    pool.wait_ge(mix_done[l], PH * (b - NS + 1))
                if s or not first:
                    pool.wait_ge(mat_ready[l], b)
                weight = att_all[l][:, bass.ds(b, 1), :].rearrange("p b k -> p (b k)").unsqueeze(2).broadcast_to([P, NE, P])
                nc.gpsimd.tensor_tensor(prod[l][:], experts[l][:], weight, ALU.mult).then_inc(pool_step, 1)
                half, n = NE // 2, 1
                while half:
                    pool.wait_ge(pool_step, done + n)
                    nc.gpsimd.tensor_tensor(prod[l][:, 0:half, :], prod[l][:, 0:half, :],
                                            prod[l][:, half:2 * half, :], ALU.add).then_inc(pool_step, 1)
                    half, n = half // 2, n + 1
                pool.wait_ge(pool_step, done + n)
                nc.gpsimd.tensor_tensor(mat[l][s][:], prod[l][:, 0, :], eye[:], ALU.add
                                        ).then_inc(mat_ready[l], 1)

            for s in range(NS):
                for l in range(2):
                    mix_matrix(l, 0, s, True)

            with pool.Fori(1, PAIRS) as i:
                for s in range(NS):
                    for l in range(2):
                        mix_matrix(l, i, s, False)

        @block.scalar
        def _(act):
            def split_x(i, s, earlier):
                b = sample(i, s)
                act.wait_ge(x_loaded[s], 16 * (i + 1))
                if earlier:
                    act.wait_ge(x_moved[s], 16 * MOVES * i)
                nc.scalar.activation(x_ph[s][:], x_in[s][:].rearrange("c (n p) -> c p n", p=PH),
                                     ACT.Copy).then_inc(x_split, 1)

            for s in range(NS):
                split_x(0, s, False)
            act.wait_ge(consts, ALL)
            for l in range(2):
                act.wait_ge(s_z, l + 1)
                nc.scalar.activation(hid[l][:, 0, :], banks[l][:, 0:NB], ACT.Gelu, bias=b0[l][:]).then_inc(s_h, 1)
            for l in range(2):
                act.wait_ge(s_z, l + 3)
                nc.scalar.activation(hid[l][:, 1, :], banks[l][:, NB:2 * NB], ACT.Gelu, bias=b1[l][:]).then_inc(s_h, 1)
            for l in range(2):
                act.wait_ge(s_att, l + 1)
                nc.scalar.activation(expo[l][:], logit[l][:], ACT.Exp, accum_out=total[l][:]).then_inc(act_step, 1)

            def body(i, last):
                act.wait_ge(bias_ready, sample(i, NS))
                for l in range(2):
                    for s in range(NS):
                        b = sample(i, s)
                        for q in range(PH):
                            act.wait_ge(conv_done[l], PH * b + q + 1)
                            nc.scalar.activation(mix_in[l][s][:, q, :], banks[PH * s + q][:], ACT.Identity,
                                                 bias=bias(s, 0 if l == 0 else 1 + G)).then_inc(mix_in_ready[l], 1)
                    if l == 0 and not last:
                        for s in range(NS):
                            split_x(i + 1, s, True)

            act.wait_ge(setup_dve, 2)
            each_pair(act, body)

        @block.vector
        def _(dve):
            count = [0]

            def step(ins):
                count[0] += 1
                ins.then_inc(dve_step, 1)
                dve.wait_ge(dve_step, count[0])

            for l in range(2):
                for s in range(NS):
                    nc.vector.memset(conv_in[l][s][:, :, 0:1], 0.0)
                    last = nc.vector.memset(conv_in[l][s][:, :, N + 1:N + 2], 0.0)
            last.then_inc(setup_dve, 1)
            dve.wait_ge(consts, ALL)
            for l in range(2):
                for g in range(G):
                    own = toep[l][:, g, :, 1, :]
                    step(nc.vector.tensor_tensor(own, own, eye[:].rearrange("p (q i) -> p q i", q=PH), ALU.add))
            for l in range(2):
                dve.wait_ge(s_z, l + 5)
                step(nc.vector.tensor_tensor(logit[l][:], banks[l][0:NB, 128:128 + NE], b2[l][:], ALU.add))
                step(nc.vector.tensor_reduce(top[l][:], logit[l][:], AX.X, ALU.max))
                nc.vector.tensor_scalar(logit[l][:], logit[l][:], top[l][:], None, ALU.subtract).then_inc(s_att, 1)
            for l in range(2):
                dve.wait_ge(act_step, l + 1)
                step(nc.vector.reciprocal(total[l][:], total[l][:]))
                step(nc.vector.tensor_scalar(att[l][:], expo[l][:], total[l][:], None, ALU.mult))
                nc.vector.tensor_tensor(att_diag[l][:], eye[0:NB, 0:NB].unsqueeze(2).broadcast_to([NB, NB, NE]),
                                        att[l][:].unsqueeze(1).broadcast_to([NB, NB, NE]), ALU.mult).then_inc(s_att, 1)
            for l in range(2):
                dve.wait_ge(s_pe, l + 1)
                nc.vector.tensor_copy(att_t[l][:], banks[2 + l][0:NE, 0:NB])
                nc.vector.tensor_copy(att_all[l][:], banks[4 + l][:, 0:NB * NE].rearrange("p (b k) -> p b k", k=NE)
                                      ).then_inc(s_att, 1)
            dve.wait_ge(s_pe, 3)
            for l, col in ((0, 0), (1, 1 + G)):
                nc.vector.tensor_scalar(biases[:, :, col], banks[6][:, NB * l:NB * (l + 1)], fside[:], None, ALU.add)
            dve.wait_ge(s_pe, 4)
            nc.vector.tensor_copy(biases[:, :, 1:1 + G],
                                  banks[7][:, 0:G * NB].rearrange("p (g b) -> p b g", g=G))
            nc.vector.tensor_copy(biases[:, :, 2 + G], banks[7][:, G * NB:(G + 1) * NB]).then_inc(setup_dve, 1)
            dve.wait_ge(setup_dve, 2)

            def body(i, last):
                if not isinstance(i, int):
                    dve.wait_ge(y_ready, PH * sample(i, 0))
                for s in range(NS):
                    nc.vector.tensor_copy(bias_now[s][:], biases[:, bass.ds(sample(i, s), 1), :].rearrange(
                        "p b c -> p (b c)")).then_inc(bias_ready, 1)
                dve.wait_ge(bias_ready, sample(i, NS))
                for s in range(NS):
                    b = sample(i, s)
                    for h in range(G):
                        dve.wait_ge(mix_done[0], G * b + h + 1)
                        nc.vector.tensor_scalar(conv_in[1][s][:, h, 1:N + 1], banks[PH * s + h][:],
                                                bias(s, 1 + h), None, ALU.add).then_inc(conv1_in_ready, 1)
                for s in range(NS):
                    b = sample(i, s)
                    dve.wait_ge(y_stored[s], 16 * i) if not isinstance(i, int) or i else None
                    for q in range(PH):
                        dve.wait_ge(mix_done[1], PH * b + q + 1)
                        nc.vector.tensor_scalar(y_out[s][:].rearrange("c (n p) -> c p n", p=PH)[:, q, :],
                                                banks[PH * s + q][:], bias(s, 2 + G), None, ALU.add
                                                ).then_inc(y_ready, 1)

            body(0, False)
            with dve.Fori(1, PAIRS) as i:
                body(i, False)

        @block.tensor
        def _(pe):
            pe.wait_ge(consts, ALL)
            for l in range(2):
                nc.tensor.matmul(banks[l][:, 0:NB], w0[l][:], cond_t[:], start=True, stop=True).then_inc(s_z, 1)
            for l in range(2):
                pe.wait_ge(s_h, l + 1)
                nc.tensor.matmul(banks[l][:, NB:2 * NB], w1[l][:], hid[l][:, 0, :], start=True, stop=True).then_inc(s_z, 1)
            for l in range(2):
                pe.wait_ge(s_h, l + 3)
                nc.tensor.matmul(banks[l][0:NB, 128:128 + NE], hid[l][:, 1, :], w2[l][:], start=True, stop=True).then_inc(s_z, 1)
            pe.wait_ge(pool_step, 1)
            for l in range(2):
                pe.wait_ge(s_att, l + 3)
                nc.tensor.matmul(banks[2 + l][0:NE, 0:NB], att[l][:], eye[0:NB, 0:NB], start=True, stop=True)
                nc.tensor.matmul(banks[4 + l][:, 0:NB * NE], ones[:], att_diag[l][:].rearrange("p b k -> p (b k)"),
                                 start=True, stop=True).then_inc(s_pe, 1)
            for l in range(2):
                last = nc.tensor.matmul(banks[6][:, NB * l:NB * (l + 1)], cw_t[l][:], cond_t[:], start=True, stop=True)
            last.then_inc(s_pe, 1)
            pe.wait_ge(s_att, 6)
            for h in range(G):
                for p in range(PH):
                    nc.tensor.matmul(banks[7][CG * p:CG * (p + 1), NB * h:NB * (h + 1)],
                                     bias_k[0][:, CG * h:CG * (h + 1)], att_t[0][:], start=True, stop=True,
                                     tile_position=(0, CG * p))
            nc.tensor.matmul(banks[7][:, G * NB:(G + 1) * NB], bias_k[1][:], att_t[1][:], start=True, stop=True
                             ).then_inc(s_pe, 1)
            pe.wait_ge(setup_dve, 2)

            def conv(l, i, s, earlier):
                b = sample(i, s)
                if l == 0:
                    pe.wait_ge(x_moved[s], 16 * MOVES * (i + 1))
                else:
                    pe.wait_ge(conv1_in_ready, G * (b + 1))
                for q in range(PH):
                    bank = banks[PH * s + q]
                    if l == 0 and earlier:
                        pe.wait_ge(y_ready, PH * (b - NS) + q + 1)
                    for m in range(REACH):
                        for g in range(G):
                            last = nc.tensor.matmul(bank[CG * g:CG * (g + 1), :], toep[l][:, g, q, m, :],
                                                    conv_in[l][s][:, g, m:m + N], start=m == 0, stop=m == REACH - 1,
                                                    tile_position=(0, CG * g))
                    last.then_inc(conv_done[l], 1)

            def mix(l, i, s):
                b = sample(i, s)
                pe.wait_ge(mat_ready[l], b + 1)
                pe.wait_ge(mix_in_ready[l], PH * (b + 1))
                for h in range(G):
                    bank = banks[PH * s + h]
                    if l == 0:
                        for p in range(PH):
                            last = nc.tensor.matmul(bank[CG * p:CG * (p + 1), :], mat[0][s][:, CG * h:CG * (h + 1)],
                                                    mix_in[0][s][:, p, :], start=True, stop=True,
                                                    tile_position=(0, CG * p))
                    else:
                        last = nc.tensor.matmul(bank[:], mat[1][s][:], mix_in[1][s][:, h, :], start=True, stop=True)
                    last.then_inc(mix_done[l], 1)

            def body(i, earlier):
                for l in range(2):
                    for s in range(NS):
                        conv(l, i, s, earlier)
                    for s in range(NS):
                        mix(l, i, s)

            body(0, False)
            with pe.Fori(1, PAIRS) as i:
                body(i, True)


def toeplitz(w):
    import numpy as np
    t = np.zeros((PH, CG, G, PH, REACH, CG), w.dtype)
    by_group = w.reshape(G, CG, CG, K)
    for p in range(PH):
        for q in range(PH):
            for m in range(REACH):
                tap = PH * (m - 1) + p - q + K // 2
                if 0 <= tap < K:
                    t[p, :, :, q, m, :] = by_group[:, :, :, tap].transpose(2, 0, 1)
    return t.reshape(P, G, PH, REACH, CG)


def kernel(**inputs):
    import numpy as np
    import concourse.bacc as bacc
    from concourse.bass_utils import run_bass_kernel_spmd

    a = {k: np.asarray(v) for k, v in inputs.items()}
    lay = {"x": a["x"], "cond_t": a["cond_128"].T, "fside": a["fside_S_0"].reshape(P, 1),
           "eye": np.eye(P, dtype=np.float32)}
    for l in range(2):
        conv, mix = f"L{2 * l}_cond_", f"L{2 * l + 1}_cond_"
        lay[f"toep{l}"] = toeplitz(a[conv + "weight"])
        lay[f"cw_t{l}"] = a[conv + "c_weight"].T
        lay[f"w0_{l}"], lay[f"w1_{l}"], lay[f"w2_{l}"] = a[mix + "W0"], a[mix + "W1"], a[mix + "W2"]
        lay[f"b0_{l}"], lay[f"b1_{l}"] = a[mix + "b0"].reshape(P, 1), a[mix + "b1"].reshape(P, 1)
        lay[f"b2_{l}"] = np.broadcast_to(a[mix + "b2"], (NB, NE))
        lay[f"experts{l}"] = a[mix + "weight"][..., 0].transpose(2, 0, 1)
        lay[f"bias_k{l}"] = a[mix + "bias_k"]
    lay = {k: np.ascontiguousarray(v) for k, v in lay.items()}
    nc = bacc.Bacc("TRN2", target_bir_lowering=False, num_devices=1)
    t = {k: nc.dram_tensor(f"in_{k}", v.shape, mybir.dt.from_np(v.dtype), kind="ExternalInput").ap()
         for k, v in lay.items()}
    out = nc.dram_tensor("out", (NB, P, L), F32, kind="ExternalOutput").ap()
    build(nc, t, out)
    r = run_bass_kernel_spmd(nc, [{f"in_{k}": v for k, v in lay.items()}], core_ids=[0])
    return r.results[0]["out"]
```

```python
from contextlib import ExitStack

import concourse.bass as bass
from concourse import mybir

F32 = mybir.dt.float32
F16 = mybir.dt.float16
I32 = mybir.dt.int32
ALU = mybir.AluOpType
ACT = mybir.ActivationFunctionType
AX = mybir.AxisListType
MAX = bass.bass_isa.ReduceOp.max

P = 128
NB = 32
L = 2048
G = 4
CG = P // G
K = 9
PH = P // CG
N = L // PH
NE = 8
REACH = 3
NS = 2
PAIRS = NB // NS
MOVES = PH * G
HI, LO = 0, 1
PASSES = ((HI, HI), (HI, LO), (LO, HI))
EXPONENT = 0x7F800000
TOP = 2.0 ** 14
TINY = 2.0 ** -60

S_X, S_MIX0, S_CONV1, S_MIX1, S_OUT, S_MORE = 0, 1, 2, 3, 4, 5
NSC = S_MORE + G - 1
B_CONV = (0, 2)
B_MIX0 = (1, 4, 5, 6)
B_MIX1 = 3
NBIAS = NSC - 1




def small_constants():
    shapes = [("cond_t0", P, NB), ("fside0", P, 1)]
    for l in range(2):
        shapes += [(f"w0_{l}", P, P), (f"b0_{l}", P, 1), (f"w1_{l}", P, P), (f"b1_{l}", P, 1), (f"w2_{l}", P, NE),
                   (f"b2_{l}", NB, NE), (f"bias_k{l}", NE, P), (f"cw_t{l}", P, P)]
    places, at = {}, 0
    for name, rows, columns in shapes:
        places[name] = (rows, columns, at)
        at += columns
    return places, at


SMALL, SMALL_COLUMNS = small_constants()


def build(nc, t, out):
    ctx = ExitStack()
    with ctx:
        def sb(name, shape, dt=F32):
            return ctx.enter_context(nc.sbuf_tensor(name, shape, dt))

        def sem(name):
            return ctx.enter_context(nc.semaphore(name))

        eye = sb("eye_sb", [P, P])
        toep = [sb(f"toep{l}", [P, G, PH, REACH, CG]) for l in range(2)]
        conv_rows = [sb(f"conv_rows{l}", [P, CG * K]) for l in range(2)]
        experts = [sb(f"experts{l}", [P, NE, P]) for l in range(2)]
        expert_rows = [sb(f"expert_rows{l}", [P, NE, P]) for l in range(2)]
        small = sb("small", [P, SMALL_COLUMNS])

        def packed(name, l=0):
            rows, columns, at = SMALL[f"{name}{l}"]
            return small[0:rows, at:at + columns]

        cond_t, fside = packed("cond_t"), packed("fside")
        cw_t, w0, w1, w2, b0, b1, b2, bias_k = ([packed(name, l) for l in range(2)] for name in
                                                ("cw_t", "w0_", "w1_", "w2_", "b0_", "b1_", "b2_", "bias_k"))
        hid = [sb(f"hid{l}", [P, 2, NB]) for l in range(2)]
        logit = [sb(f"logit{l}", [NB, NE]) for l in range(2)]
        top = [sb(f"top{l}", [NB, 1]) for l in range(2)]
        expo = [sb(f"expo{l}", [NB, NE]) for l in range(2)]
        total = [sb(f"total{l}", [NB, 1]) for l in range(2)]
        att = [sb(f"att{l}", [NB, NE]) for l in range(2)]
        att_diag = [sb(f"att_diag{l}", [NB, NB, NE]) for l in range(2)]
        att_t = [sb(f"att_t{l}", [NE, NB]) for l in range(2)]
        ones = sb("ones", [NB, P])
        att_all = [sb(f"att_all{l}", [P, NB, NE]) for l in range(2)]
        eye_scaled = [sb(f"eye_scaled{l}", [P, P]) for l in range(2)]
        toep_half = [sb(f"toep_half{l}", [P, 2, G, PH, REACH, CG], F16) for l in range(2)]
        biases = sb("biases", [P, NB, NBIAS])
        row_top = sb("row_top", [P, 2, NE])
        first_row = sb("first_row", [P, 1])
        first_row_all = sb("first_row_all", [P, 1])
        stats = sb("stats", [P, 6])
        stats_all = sb("stats_all", [P, 6])
        weight_scale = sb("weight_scale", [P, 4])
        weight_undo = sb("weight_undo", [P, 4])
        grow = sb("grow", [P, NSC])
        shift = sb("shift", [P, NSC])
        x_in = [sb(f"x_in{s}", [P, L]) for s in range(NS)]
        x_max = [sb(f"x_max{s}", [P, 1]) for s in range(NS)]
        x_seen = [sb(f"x_seen{s}", [P, 1]) for s in range(NS)]
        x_all = [sb(f"x_all{s}", [P, 1]) for s in range(NS)]
        bound = [sb(f"bound{s}", [P, NSC]) for s in range(NS)]
        power = [sb(f"power{s}", [P, NSC]) for s in range(NS)]
        scale = [sb(f"scale{s}", [P, NSC]) for s in range(NS)]
        factor = [sb(f"factor{s}", [P, 4]) for s in range(NS)]
        affine_next = [sb(f"affine_next{s}", [P, 4 + NBIAS]) for s in range(NS)]
        affine = [sb(f"affine{s}", [P, 4 + NBIAS]) for s in range(NS)]
        x_ph = [sb(f"x_ph{s}", [P, 2, PH, N], F16) for s in range(NS)]
        conv_in = [[sb(f"conv_in{l}_{s}", [P, 2, G, N + 2], F16) for s in range(NS)] for l in range(2)]
        mix_in = [[sb(f"mix_in{l}_{s}", [P, 2, PH, N], F16) for s in range(NS)] for l in range(2)]
        value = [sb(f"value{s}", [P, 4, N]) for s in range(NS)]
        y_out = [sb(f"y_out{s}", [P, L]) for s in range(NS)]
        prod = [sb(f"prod{l}", [P, NE, P]) for l in range(2)]
        mat = [sb(f"mat{l}", [P, P]) for l in range(2)]
        mat_half = [[sb(f"mat_half{l}_{s}", [P, 2, P], F16) for s in range(NS)] for l in range(2)]
        banks = [ctx.enter_context(nc.psum_tensor(f"bank{i}", [P, N], F32)) for i in range(8)]

        load_rest = [(expert_rows[0], t["expert_rows0"]), (conv_rows[1], t["conv_rows1"]),
                     (expert_rows[1], t["expert_rows1"]), (toep[1], t["toep1"]), (experts[0], t["experts0"]),
                     (experts[1], t["experts1"])]

        toep_loaded = sem("toep_loaded")
        small_loaded = sem("small_loaded")
        rest_loaded = sem("rest_loaded")
        rows_loaded = sem("rows_loaded")
        scale_ready = sem("weight_scale_ready")
        toep_high = sem("toep_high")
        REST = 16 * len(load_rest)
        x_loaded = [sem(f"x_loaded{s}") for s in range(NS)]
        x_max_ready = sem("x_max_ready")
        x_all_ready = sem("x_all_ready")
        x_scale_ready = sem("x_scale_ready")
        x_high = sem("x_high")
        x_split = sem("x_split")
        x_moved = [sem(f"x_moved{s}") for s in range(NS)]
        affine_ready = sem("affine_ready")
        product = [sem(f"product{k}") for k in range(4)]
        valued = [sem(f"valued{k}") for k in range(3)]
        split = [sem(f"split{k}") for k in range(3)]
        y_ready = sem("y_ready")
        y_stored = [sem(f"y_stored{s}") for s in range(NS)]
        mat_ready = [sem(f"mat_ready{l}") for l in range(2)]
        pool_step = sem("pool_step")
        dve_step = sem("dve_step")
        ones_ready = sem("ones_ready")
        borders_zero = sem("borders_zero")
        first_row_ready = sem("first_row_ready")
        first_row_reduced = sem("first_row_reduced")
        toep_ready = sem("toep_ready")
        stats_ready = sem("stats_ready")
        stats_reduced = sem("stats_reduced")
        att_all_ready = sem("att_all_ready")
        router_product = sem("router_product")
        router_hidden = sem("router_hidden")
        logit_ready = sem("logit_ready")
        exp_ready = sem("exp_ready")
        att_ready = sem("att_ready")
        att_t_ready = sem("att_t_ready")
        spread_product = sem("spread_product")
        conv_bias_product = sem("conv_bias_product")
        mix_bias_product = sem("mix_bias_product")

        def sample(i, s):
            return i * NS + s

        def repeats(i):
            return not isinstance(i, int) or i > 0

        def layer_input(k, s):
            return conv_in[1][s][:, :, :, 1:N + 1] if k == 1 else mix_in[k // 2][s][:]

        block = ctx.enter_context(nc.Block())

        @block.sync
        def _(sp):
            def load_x(b, s):
                sp.dma_start(x_in[s][:], t["x"][bass.ds(b, 1), :, :].rearrange("b c l -> (b c) l")
                             ).then_inc(x_loaded[s], 16)

            def move_x(i, s):
                sp.wait_ge(x_split, sample(i, s) + 1)
                for p in range(PH):
                    for g in range(G):
                        sp.dma_start(conv_in[0][s][CG * p:CG * (p + 1), :, g, 1:N + 1],
                                     x_ph[s][CG * g:CG * (g + 1), :, p, :]).then_inc(x_moved[s], 16)

            sp.dma_start(conv_rows[0][:], t["conv_rows0"]).then_inc(rows_loaded, 16)
            load_x(0, 0)
            sp.dma_start(eye[:], t["eye"]).then_inc(toep_loaded, 16)
            sp.dma_start(toep[0][:], t["toep0"]).then_inc(toep_loaded, 16)
            sp.dma_start(small[:], t["small"]).then_inc(small_loaded, 16)
            load_x(1, 1)
            for dst, src in load_rest:
                sp.dma_start(dst[:], src).then_inc(rest_loaded, 16)
            sp.wait_ge(borders_zero, 1)
            for s in range(NS):
                move_x(0, s)
                load_x(NS + s, s)

            def pair(i, last, load=False):
                if not last:
                    for s in range(NS):
                        move_x(i + 1, s)
                        if load:
                            load_x(sample(i + 2, s), s)
                for s in range(NS):
                    b = sample(i, s)
                    sp.wait_ge(y_ready, PH * (b + 1))
                    sp.dma_start(out[bass.ds(b, 1), :, :].rearrange("b c l -> (b c) l"), y_out[s][:]
                                 ).then_inc(y_stored[s], 16)

            with sp.Fori(0, PAIRS - 2) as i:
                pair(i, False, load=True)
            pair(PAIRS - 2, False)
            pair(PAIRS - 1, True)
            for s in range(NS):
                sp.wait_ge(y_stored[s], 16 * PAIRS)

        @block.gpsimd
        def _(pool):
            SUMS = 5

            def all_reduce(i, s):
                b = sample(i, s)
                pool.wait_ge(x_max_ready, b + 1)
                nc.gpsimd.tensor_tensor(x_seen[s][:], x_max[s][:], x_max[s][:], ALU.add)
                nc.gpsimd.partition_all_reduce(x_all[s][:], x_max[s][:], P, MAX).then_inc(x_all_ready, 1)

            def mix_matrix(l, i, s):
                b = sample(i, s)
                done = (i * 2 * NS + l * NS + s) * SUMS
                if s or repeats(i):
                    pool.wait_ge(mat_ready[l], b)
                weight = att_all[l][:, bass.ds(b, 1), :].rearrange("p b k -> p (b k)").unsqueeze(2).broadcast_to([P, NE, P])
                nc.gpsimd.tensor_tensor(prod[l][:], experts[l][:], weight, ALU.mult).then_inc(pool_step, 1)
                half, n = NE // 2, 1
                while half:
                    pool.wait_ge(pool_step, done + n)
                    nc.gpsimd.tensor_tensor(prod[l][:, 0:half, :], prod[l][:, 0:half, :],
                                            prod[l][:, half:2 * half, :], ALU.add).then_inc(pool_step, 1)
                    half, n = half // 2, n + 1
                if repeats(i):
                    pool.wait_ge(product[2 * l + 1], PH * (b - NS + 1))
                pool.wait_ge(pool_step, done + n)
                nc.gpsimd.tensor_tensor(mat_half[l][s][:, HI, :], prod[l][:, 0, :], eye_scaled[l][:], ALU.add)
                nc.gpsimd.tensor_tensor(mat[l][:], prod[l][:, 0, :], eye_scaled[l][:], ALU.add).then_inc(pool_step, 1)
                pool.wait_ge(pool_step, done + n + 1)
                nc.gpsimd.tensor_tensor(mat_half[l][s][:, LO, :], mat[l][:], mat_half[l][s][:, HI, :], ALU.subtract
                                        ).then_inc(mat_ready[l], 1)

            nc.gpsimd.memset(ones[:], 1.0).then_inc(ones_ready, 1)
            pool.wait_ge(first_row_ready, 1)
            nc.gpsimd.partition_all_reduce(first_row_all[:], first_row[:], P, MAX).then_inc(first_row_reduced, 1)
            for s in range(NS):
                all_reduce(0, s)
            pool.wait_ge(stats_ready, 1)
            nc.gpsimd.partition_all_reduce(stats_all[:], stats[:], P, MAX).then_inc(stats_reduced, 1)
            pool.wait_ge(att_all_ready, 1)
            for l in range(2):
                for s in range(NS):
                    mix_matrix(l, 0, s)

            with pool.Fori(1, PAIRS) as i:
                for s in range(NS):
                    all_reduce(i, s)
                for l in range(2):
                    for s in range(NS):
                        mix_matrix(l, i, s)

        @block.scalar
        def _(act):
            def high_x(i, s):
                b = sample(i, s)
                act.wait_ge(x_scale_ready, b + 1)
                if repeats(i):
                    act.wait_ge(x_moved[s], 16 * MOVES * i)
                nc.scalar.activation(x_ph[s][:, HI, :, :], x_in[s][:].rearrange("c (n p) -> c p n", p=PH),
                                     ACT.Identity, scale=scale[s][:, S_X:S_X + 1]).then_inc(x_high, 1)

            def evacuate(k, i, s, qs=range(4)):
                b = sample(i, s)
                for q in qs:
                    act.wait_ge(product[k], 4 * b + q + 1)
                    if k < 3:
                        dst, done = value[s][:, q, :], valued[k]
                    else:
                        dst, done = y_out[s][:].rearrange("c (n p) -> c p n", p=PH)[:, q, :], y_ready
                    col = 4 + (B_CONV[0], B_MIX0[q], B_CONV[1], B_MIX1)[k]
                    nc.scalar.activation(dst, banks[4 * s + q][:], ACT.Identity, bias=affine[s][:, col:col + 1],
                                         scale=affine[s][:, k:k + 1]).then_inc(done, 1)

            high_x(0, 0)
            act.wait_ge(small_loaded, 16)
            for l in range(2):
                act.wait_ge(router_product, l + 1)
                nc.scalar.activation(hid[l][:, 0, :], banks[4 + l][:, 0:NB], ACT.Gelu, bias=b0[l]).then_inc(router_hidden, 1)
            for l in range(2):
                act.wait_ge(router_product, l + 3)
                nc.scalar.activation(hid[l][:, 1, :], banks[4 + l][:, NB:2 * NB], ACT.Gelu, bias=b1[l]).then_inc(router_hidden, 1)
            for l in range(2):
                act.wait_ge(logit_ready, l + 1)
                nc.scalar.activation(expo[l][:], logit[l][:], ACT.Exp, accum_out=total[l][:]).then_inc(exp_ready, 1)
            high_x(0, 1)
            act.wait_ge(scale_ready, 1)
            nc.scalar.activation(toep_half[1][:, HI].rearrange("p g q m c -> p (g q m c)"),
                                 toep[1][:].rearrange("p g q m c -> p (g q m c)"), ACT.Identity,
                                 scale=weight_scale[:, 2:3]).then_inc(toep_high, 1)

            def body(i, last):
                act.wait_ge(affine_ready, sample(i, NS))
                for s in range(NS):
                    evacuate(0, i, s)
                for s in range(NS):
                    evacuate(1, i, s)
                for s in range(NS):
                    evacuate(2, i, s, (0,))
                    if not last:
                        high_x(i + 1, s)
                    evacuate(2, i, s, (1, 2, 3))
                for s in range(NS):
                    if repeats(i):
                        act.wait_ge(y_stored[s], 16 * i)
                    evacuate(3, i, s)

            body(0, False)
            with act.Fori(1, PAIRS - 1) as i:
                body(i, False)
            body(PAIRS - 1, True)

        @block.vector
        def _(dve):
            before, made = [0], [0]
            PER_TURN = 3 * NS * 4 + NS * 2 + NS * 5

            def step(ins, i=0):
                made[0] += 1
                ins.then_inc(dve_step, 1)
                dve.wait_ge(dve_step, before[0] + made[0] + PER_TURN * i)

            def largest_x(i, s):
                dve.wait_ge(x_loaded[s], 16 * (i + 1))
                nc.vector.tensor_reduce(x_max[s][:], x_in[s][:], AX.X, ALU.max, apply_absolute_value=True
                                        ).then_inc(x_max_ready, 1)

            def scale_x(i, s, turn):
                dve.wait_ge(x_all_ready, sample(i, s) + 1)
                step(nc.vector.tensor_scalar(bound[s][:, S_X:S_X + 1], x_all[s][:], 1 / TOP, TINY, ALU.mult, ALU.max), turn)
                step(nc.vector.tensor_scalar(power[s][:, S_X:S_X + 1].bitcast(I32), bound[s][:, S_X:S_X + 1].bitcast(I32),
                                             EXPONENT, None, ALU.bitwise_and), turn)
                nc.vector.reciprocal(scale[s][:, S_X:S_X + 1], power[s][:, S_X:S_X + 1]).then_inc(x_scale_ready, 1)

            def low_x(i, s):
                dve.wait_ge(x_high, sample(i, s) + 1)
                nc.vector.scalar_tensor_tensor(x_ph[s][:, LO, :, :], x_in[s][:].rearrange("c (n p) -> c p n", p=PH),
                                               scale[s][:, S_X:S_X + 1], x_ph[s][:, HI, :, :], ALU.mult, ALU.subtract
                                               ).then_inc(x_split, 1)

            def scale_values(i, s, turn):
                b = sample(i, s)
                rest = slice(S_X + 1, NSC)
                step(nc.vector.scalar_tensor_tensor(bound[s][:, rest], grow[:, rest], bound[s][:, S_X:S_X + 1],
                                                    shift[:, rest], ALU.mult, ALU.add), turn)
                step(nc.vector.tensor_scalar(power[s][:, rest].bitcast(I32), bound[s][:, rest].bitcast(I32), EXPONENT,
                                             None, ALU.bitwise_and), turn)
                step(nc.vector.reciprocal(scale[s][:, rest], power[s][:, rest]), turn)
                step(nc.vector.tensor_tensor(factor[s][:], power[s][:, 0:4], weight_undo[:], ALU.mult), turn)
                nc.vector.tensor_tensor(affine_next[s][:, 0:4], scale[s][:, 1:5], factor[s][:], ALU.mult)
                step(nc.vector.tensor_tensor(affine_next[s][:, 4:4 + NBIAS], scale[s][:, rest],
                                             biases[:, bass.ds(b, 1), :].rearrange("p b c -> p (b c)"), ALU.mult), turn)

            def halve(k, i, s, qs=range(4)):
                b = sample(i, s)
                for q in qs:
                    dve.wait_ge(valued[k], 4 * b + q + 1)
                    step(nc.vector.tensor_copy(layer_input(k, s)[:, HI, q, :], value[s][:, q, :]), i)
                    nc.vector.tensor_tensor(layer_input(k, s)[:, LO, q, :], value[s][:, q, :],
                                            layer_input(k, s)[:, HI, q, :], ALU.subtract).then_inc(split[k], 1)

            def halve_toep(l):
                high, low = (toep_half[l][:, h].rearrange("p g q m c -> p (g q m c)") for h in (HI, LO))
                whole = toep[l][:].rearrange("p g q m c -> p (g q m c)")
                by = weight_scale[:, 2 * l:2 * l + 1]
                if l == 0:
                    step(nc.vector.tensor_scalar(high, whole, by, None, ALU.mult))
                else:
                    dve.wait_ge(toep_high, 1)
                nc.vector.scalar_tensor_tensor(low, whole, by, high, ALU.mult, ALU.subtract).then_inc(toep_ready, 1)

            def add_residual(l):
                for g in range(G):
                    own = toep[l][:, g, :, 1, :]
                    ins = nc.vector.tensor_tensor(own, own, eye[:].rearrange("p (q i) -> p q i", q=PH), ALU.add)
                step(ins)

            for l in range(2):
                for s in range(NS):
                    nc.vector.memset(conv_in[l][s][:, :, :, 0:1], 0.0)
                    last = nc.vector.memset(conv_in[l][s][:, :, :, N + 1:N + 2], 0.0)
            last.then_inc(borders_zero, 1)
            dve.wait_ge(rows_loaded, 16)
            nc.vector.tensor_reduce(first_row[:], conv_rows[0][:], AX.X, ALU.add, apply_absolute_value=True
                                    ).then_inc(first_row_ready, 1)
            largest_x(0, 0)
            dve.wait_ge(first_row_reduced, 1)
            step(nc.vector.tensor_scalar(first_row_all[:], first_row_all[:], 1.0, None, ALU.add))
            step(nc.vector.tensor_scalar(weight_undo[:, 0:1], first_row_all[:], 1 / TOP, None, ALU.mult))
            step(nc.vector.tensor_scalar(weight_undo[:, 0:1].bitcast(I32), weight_undo[:, 0:1].bitcast(I32), EXPONENT,
                                         None, ALU.bitwise_and))
            step(nc.vector.reciprocal(weight_scale[:, 0:1], weight_undo[:, 0:1]))
            scale_x(0, 0, 0)
            dve.wait_ge(toep_loaded, 32)
            add_residual(0)
            low_x(0, 0)
            halve_toep(0)
            dve.wait_ge(small_loaded, 16)
            for l in range(2):
                dve.wait_ge(router_product, l + 5)
                step(nc.vector.tensor_tensor(logit[l][:], banks[4 + l][0:NB, 128:128 + NE], b2[l], ALU.add))
                step(nc.vector.tensor_reduce(top[l][:], logit[l][:], AX.X, ALU.max))
                nc.vector.tensor_scalar(logit[l][:], logit[l][:], top[l][:], None, ALU.subtract).then_inc(logit_ready, 1)
            largest_x(0, 1)
            for l in range(2):
                dve.wait_ge(exp_ready, l + 1)
                step(nc.vector.reciprocal(total[l][:], total[l][:]))
                step(nc.vector.tensor_scalar(att[l][:], expo[l][:], total[l][:], None, ALU.mult))
                nc.vector.tensor_tensor(att_diag[l][:], eye[0:NB, 0:NB].unsqueeze(2).broadcast_to([NB, NB, NE]),
                                        att[l][:].unsqueeze(1).broadcast_to([NB, NB, NE]), ALU.mult).then_inc(att_ready, 1)
            scale_x(0, 1, 0)
            for l in range(2):
                dve.wait_ge(spread_product, l + 1)
                nc.vector.tensor_copy(att_t[l][:], banks[4 + l][0:NE, 160:160 + NB]).then_inc(att_t_ready, 1)
            low_x(0, 1)
            dve.wait_ge(rest_loaded, REST)
            add_residual(1)
            for l in range(2):
                ins = nc.vector.tensor_reduce(row_top[:, l, :], expert_rows[l][:], AX.X, ALU.add,
                                              apply_absolute_value=True)
            step(ins)
            for l in range(2):
                nc.vector.tensor_reduce(stats[:, 2 * l:2 * l + 1], row_top[:, l, :], AX.X, ALU.max)
            nc.vector.tensor_reduce(stats[:, 1:2], conv_rows[1][:], AX.X, ALU.add, apply_absolute_value=True)
            dve.wait_ge(conv_bias_product, 1)
            for l in range(2):
                nc.vector.tensor_scalar(biases[:, :, B_CONV[l]], banks[6][:, NB * l:NB * (l + 1)], fside, None, ALU.add)
            dve.wait_ge(mix_bias_product, 1)
            for h in range(G):
                nc.vector.tensor_copy(biases[:, :, B_MIX0[h]], banks[7][:, NB * h:NB * (h + 1)])
            step(nc.vector.tensor_copy(biases[:, :, B_MIX1], banks[7][:, G * NB:(G + 1) * NB]))
            for col, b in ((3, B_CONV[0]), (5, B_CONV[1])):
                nc.vector.tensor_reduce(stats[:, col:col + 1], biases[:, :, b], AX.X, ALU.max, apply_absolute_value=True)
            nc.vector.tensor_reduce(stats[:, 4:5], banks[7][:, 0:G * NB], AX.X, ALU.max, apply_absolute_value=True
                                    ).then_inc(stats_ready, 1)
            dve.wait_ge(stats_reduced, 1)
            nc.vector.tensor_scalar(stats_all[:, 3:6], stats_all[:, 3:6], 1 / TOP, None, ALU.mult)
            step(nc.vector.tensor_scalar(stats_all[:, 0:3], stats_all[:, 0:3], 1.0, None, ALU.add))
            step(nc.vector.tensor_scalar(weight_undo[:, 1:4], stats_all[:, 0:3], 1 / TOP, None, ALU.mult))
            step(nc.vector.tensor_scalar(weight_undo[:, 1:4].bitcast(I32), weight_undo[:, 1:4].bitcast(I32), EXPONENT,
                                         None, ALU.bitwise_and))
            step(nc.vector.reciprocal(weight_scale[:, 1:4], weight_undo[:, 1:4]))
            nc.vector.drain().then_inc(scale_ready, 1)
            for l in range(2):
                by = weight_scale[:, 2 * l + 1:2 * l + 2]
                nc.vector.tensor_scalar(eye_scaled[l][:], eye[:], by, None, ALU.mult)
                last = nc.vector.tensor_scalar(att_all[l][:], banks[4 + l][:, 256:512].rearrange("p (b k) -> p b k", k=NE),
                                               by, None, ALU.mult)
            last.then_inc(att_all_ready, 1)
            row0, row1, row2 = first_row_all[:], stats_all[:, 0:1], stats_all[:, 1:2]
            more = slice(S_MORE, NSC)
            nc.vector.memset(grow[:, S_OUT:S_OUT + 1], 0.0)
            nc.vector.memset(shift[:, S_OUT:S_OUT + 1], 1.0)
            nc.vector.tensor_copy(grow[:, S_MIX0:S_MIX0 + 1], row0)
            nc.vector.tensor_copy(shift[:, S_MIX0:S_MIX0 + 1], stats_all[:, 3:4])
            nc.vector.tensor_tensor(grow[:, S_CONV1:S_CONV1 + 1], row0, row1, ALU.mult)
            step(nc.vector.tensor_scalar(shift[:, S_CONV1:S_CONV1 + 1], stats_all[:, 3:4], row1, stats_all[:, 4:5],
                                         ALU.mult, ALU.add))
            nc.vector.tensor_tensor(grow[:, S_MIX1:S_MIX1 + 1], grow[:, S_CONV1:S_CONV1 + 1], row2, ALU.mult)
            nc.vector.tensor_scalar(shift[:, S_MIX1:S_MIX1 + 1], shift[:, S_CONV1:S_CONV1 + 1], row2, stats_all[:, 5:6],
                                    ALU.mult, ALU.add)
            for a in (grow, shift):
                last = nc.vector.tensor_copy(a[:, more], a[:, S_CONV1:S_CONV1 + 1].broadcast_to([P, G - 1]))
            step(last)
            for s in range(NS):
                scale_values(0, s, 0)
            before[0], made[0] = made[0], 0

            def body(i, last):
                made[0] = 0
                if repeats(i):
                    dve.wait_ge(y_ready, 4 * sample(i, 0))
                for s in range(NS):
                    nc.vector.tensor_copy(affine[s][:], affine_next[s][:]).then_inc(affine_ready, 1)
                if not repeats(i):
                    halve_toep(1)
                for s in range(NS):
                    halve(0, i, s, (0,))
                    if not last:
                        largest_x(i + 1, s)
                    halve(0, i, s, (1, 2, 3))
                for s in range(NS):
                    halve(1, i, s)
                if not last:
                    for s in range(NS):
                        scale_x(i + 1, s, i)
                for s in range(NS):
                    halve(2, i, s, (0,))
                    if not last:
                        low_x(i + 1, s)
                    halve(2, i, s, (1,))
                    if not last:
                        scale_values(i + 1, s, i)
                    halve(2, i, s, (2, 3))
                if not last:
                    assert made[0] == PER_TURN

            body(0, False)
            with dve.Fori(1, PAIRS - 1) as i:
                body(i, False)
            body(PAIRS - 1, True)

        @block.tensor
        def _(pe):
            def conv_bank(l, s, q):
                bank = banks[4 * s + q]
                n = 0
                for m in range(REACH):
                    for w, x in PASSES:
                        for g in range(G):
                            last = nc.tensor.matmul(bank[CG * g:CG * (g + 1), :], toep_half[l][:, w, g, q, m, :],
                                                    conv_in[l][s][:, x, g, m:m + N], start=n == 0,
                                                    stop=n == REACH * len(PASSES) - 1, tile_position=(0, CG * g))
                        n += 1
                last.then_inc(product[2 * l], 1)

            def conv(l, i, s):
                b = sample(i, s)
                if l == 0:
                    pe.wait_ge(x_moved[s], 16 * MOVES * (i + 1))
                else:
                    pe.wait_ge(split[1], 4 * (b + 1))
                for q in range(PH):
                    if l == 0 and repeats(i):
                        pe.wait_ge(y_ready, 4 * (b - NS) + q + 1)
                    conv_bank(l, s, q)

            def mix(l, i, s):
                b = sample(i, s)
                pe.wait_ge(mat_ready[l], b + 1)
                pe.wait_ge(split[2 * l], 4 * (b + 1))
                for h in range(G):
                    bank = banks[4 * s + h]
                    for n, (w, x) in enumerate(PASSES):
                        flags = dict(start=n == 0, stop=n == len(PASSES) - 1)
                        if l == 0:
                            for p in range(PH):
                                last = nc.tensor.matmul(bank[CG * p:CG * (p + 1), :],
                                                        mat_half[0][s][:, w, CG * h:CG * (h + 1)],
                                                        mix_in[0][s][:, x, p, :], tile_position=(0, CG * p), **flags)
                        else:
                            last = nc.tensor.matmul(bank[:], mat_half[1][s][:, w, :], mix_in[1][s][:, x, h, :], **flags)
                    last.then_inc(product[2 * l + 1], 1)

            pe.wait_ge(small_loaded, 16)
            for l in range(2):
                nc.tensor.matmul(banks[4 + l][:, 0:NB], w0[l], cond_t, start=True, stop=True).then_inc(router_product, 1)
            for l in range(2):
                last = nc.tensor.matmul(banks[6][:, NB * l:NB * (l + 1)], cw_t[l], cond_t, start=True, stop=True)
            last.then_inc(conv_bias_product, 1)
            for l in range(2):
                pe.wait_ge(router_hidden, l + 1)
                nc.tensor.matmul(banks[4 + l][:, NB:2 * NB], w1[l], hid[l][:, 0, :], start=True, stop=True
                                 ).then_inc(router_product, 1)
            for l in range(2):
                pe.wait_ge(router_hidden, l + 3)
                nc.tensor.matmul(banks[4 + l][0:NB, 128:128 + NE], hid[l][:, 1, :], w2[l], start=True, stop=True
                                 ).then_inc(router_product, 1)
            pe.wait_ge(toep_loaded, 32)
            pe.wait_ge(ones_ready, 1)
            for l in range(2):
                pe.wait_ge(att_ready, l + 1)
                nc.tensor.matmul(banks[4 + l][0:NE, 160:160 + NB], att[l][:], eye[0:NB, 0:NB], start=True, stop=True)
                nc.tensor.matmul(banks[4 + l][:, 256:512], ones[:], att_diag[l][:].rearrange("p b k -> p (b k)"),
                                 start=True, stop=True).then_inc(spread_product, 1)
            pe.wait_ge(att_t_ready, 2)
            for h in range(G):
                for p in range(PH):
                    nc.tensor.matmul(banks[7][CG * p:CG * (p + 1), NB * h:NB * (h + 1)],
                                     bias_k[0][:, CG * h:CG * (h + 1)], att_t[0][:], start=True, stop=True,
                                     tile_position=(0, CG * p))
            nc.tensor.matmul(banks[7][:, G * NB:(G + 1) * NB], bias_k[1], att_t[1][:], start=True, stop=True
                             ).then_inc(mix_bias_product, 1)
            pe.wait_ge(borders_zero, 1)
            pe.wait_ge(toep_ready, 1)
            conv(0, 0, 0)
            pe.wait_ge(att_all_ready, 1)
            conv(0, 0, 1)

            def body(i, first):
                for l in range(2):
                    if l or not first:
                        if l:
                            pe.wait_ge(toep_ready, 2)
                        for s in range(NS):
                            conv(l, i, s)
                    for s in range(NS):
                        mix(l, i, s)

            body(0, True)
            with pe.Fori(1, PAIRS) as i:
                body(i, False)


def toeplitz(w):
    import numpy as np
    t = np.zeros((PH, CG, G, PH, REACH, CG), w.dtype)
    by_group = w.reshape(G, CG, CG, K)
    for p in range(PH):
        for q in range(PH):
            for m in range(REACH):
                tap = PH * (m - 1) + p - q + K // 2
                if 0 <= tap < K:
                    t[p, :, :, q, m, :] = by_group[:, :, :, tap].transpose(2, 0, 1)
    return t.reshape(P, G, PH, REACH, CG)


def kernel(**inputs):
    import numpy as np
    import concourse.bacc as bacc
    from concourse.bass_utils import run_bass_kernel_spmd

    a = {k: np.asarray(v) for k, v in inputs.items()}
    lay = {"x": a["x"], "eye": np.eye(P, dtype=np.float32)}
    small = {"cond_t0": a["cond_128"].T, "fside0": a["fside_S_0"].reshape(P, 1)}
    for l in range(2):
        conv, mix = f"L{2 * l}_cond_", f"L{2 * l + 1}_cond_"
        lay[f"toep{l}"] = toeplitz(a[conv + "weight"])
        lay[f"conv_rows{l}"] = a[conv + "weight"].reshape(P, CG * K)
        lay[f"experts{l}"] = a[mix + "weight"][..., 0].transpose(2, 0, 1)
        lay[f"expert_rows{l}"] = a[mix + "weight"][..., 0].transpose(1, 0, 2)
        small[f"cw_t{l}"] = a[conv + "c_weight"].T
        small[f"w0_{l}"], small[f"w1_{l}"], small[f"w2_{l}"] = a[mix + "W0"], a[mix + "W1"], a[mix + "W2"]
        small[f"b0_{l}"], small[f"b1_{l}"] = a[mix + "b0"].reshape(P, 1), a[mix + "b1"].reshape(P, 1)
        small[f"b2_{l}"] = np.broadcast_to(a[mix + "b2"], (NB, NE))
        small[f"bias_k{l}"] = a[mix + "bias_k"]
    lay["small"] = np.zeros((P, SMALL_COLUMNS), np.float32)
    for name, (rows, columns, at) in SMALL.items():
        lay["small"][:rows, at:at + columns] = small[name]
    lay = {k: np.ascontiguousarray(v) for k, v in lay.items()}
    nc = bacc.Bacc("TRN2", target_bir_lowering=False, num_devices=1)
    t = {k: nc.dram_tensor(f"in_{k}", v.shape, mybir.dt.from_np(v.dtype), kind="ExternalInput").ap()
         for k, v in lay.items()}
    out = nc.dram_tensor("out", (NB, P, L), F32, kind="ExternalOutput").ap()
    build(nc, t, out)
    r = run_bass_kernel_spmd(nc, [{f"in_{k}": v for k, v in lay.items()}], core_ids=[0])
    return r.results[0]["out"]
```

```python
from contextlib import ExitStack

import concourse.bass as bass
from concourse import mybir

F32 = mybir.dt.float32
F16 = mybir.dt.float16
I32 = mybir.dt.int32
ALU = mybir.AluOpType
ACT = mybir.ActivationFunctionType
AX = mybir.AxisListType
MAX = bass.bass_isa.ReduceOp.max

P = 128
NB = 32
L = 2048
G = 4
CG = P // G
K = 9
PH = P // CG
N = L // PH
NE = 8
REACH = 3
NS = 2
A, B = 0, 1
PAIRS = NB // NS
MOVES = G
HI, LO = 0, 1
PASSES = ((HI, HI), (HI, LO), (LO, HI))
EXPONENT = 0x7F800000
TOP = 2.0 ** 14
TINY = 2.0 ** -60

S_X, S_MIX0, S_CONV1, S_MIX1, S_OUT = range(5)
S_MORE = {S_MIX0: 5, S_CONV1: 5 + (G - 1), S_MIX1: 5 + 2 * (G - 1)}
NSC = 5 + 3 * (G - 1)
NBIAS = NSC - 1


def bias_column(k, q):
    return k if k == 3 or q == 0 else S_MORE[k + 1] - 1 + q - 1


def small_constants():
    shapes = [("cond_t0", P, NB), ("fside0", P, G)]
    for l in range(2):
        shapes += [(f"w0_{l}", P, P), (f"b0_{l}", P, 1), (f"w1_{l}", P, P), (f"b1_{l}", P, 1), (f"w2_{l}", P, NE),
                   (f"b2_{l}", NB, NE), (f"bias_k{l}", NE, P), (f"cw_t{l}", P, G * P)]
    places, at = {}, 0
    for name, rows, columns in shapes:
        places[name] = (rows, columns, at)
        at += columns
    return places, at


SMALL, SMALL_COLUMNS = small_constants()


def build(nc, t, out):
    ctx = ExitStack()
    with ctx:
        def sb(name, shape, dt=F32):
            return ctx.enter_context(nc.sbuf_tensor(name, shape, dt))

        def sem(name):
            return ctx.enter_context(nc.semaphore(name))

        eye = sb("eye_sb", [P, P])
        eye_phases = sb("eye_phases_sb", [P, P])
        toep = [sb(f"toep{l}", [P, G, REACH, P]) for l in range(2)]
        conv_rows = [sb(f"conv_rows{l}", [P, CG * K]) for l in range(2)]
        experts = [sb(f"experts{l}", [P, NE, P]) for l in range(2)]
        small = sb("small", [P, SMALL_COLUMNS])

        def packed(name, l=0):
            rows, columns, at = SMALL[f"{name}{l}"]
            return small[0:rows, at:at + columns]

        cond_t, fside = packed("cond_t"), packed("fside")
        cw_t, w0, w1, w2, b0, b1, b2, bias_k = ([packed(name, l) for l in range(2)] for name in
                                                ("cw_t", "w0_", "w1_", "w2_", "b0_", "b1_", "b2_", "bias_k"))
        hid = [sb(f"hid{l}", [P, 2, NB]) for l in range(2)]
        logit = [sb(f"logit{l}", [NB, NE]) for l in range(2)]
        top = [sb(f"top{l}", [NB, 1]) for l in range(2)]
        expo = [sb(f"expo{l}", [NB, NE]) for l in range(2)]
        total = [sb(f"total{l}", [NB, 1]) for l in range(2)]
        att = [sb(f"att{l}", [NB, NE]) for l in range(2)]
        att_diag = [sb(f"att_diag{l}", [NB, NB, NE]) for l in range(2)]
        att_t = [sb(f"att_t{l}", [NE, NB]) for l in range(2)]
        ones = sb("ones", [NB, P])
        att_all = [sb(f"att_all{l}", [P, NB, NE]) for l in range(2)]
        eye_scaled = [sb(f"eye_scaled{l}", [P, P]) for l in range(2)]
        toep_half = [sb(f"toep_half{l}", [P, 2, G, REACH, P], F16) for l in range(2)]
        conv_bias = [sb(f"conv_bias{l}", [P, G, NB]) for l in range(2)]
        biases = sb("biases", [P, NB, NBIAS])
        row_top = sb("row_top", [P, 2, NE])
        first_row = sb("first_row", [P, 1])
        first_row_all = sb("first_row_all", [P, 1])
        stats = sb("stats", [P, 6])
        stats_all = sb("stats_all", [P, 6])
        weight_scale = sb("weight_scale", [P, 4])
        weight_undo = sb("weight_undo", [P, 4])
        grow = sb("grow", [P, NSC])
        shift = sb("shift", [P, NSC])
        x_in = [sb(f"x_in{s}", [P, L]) for s in range(NS)]
        x_max = [sb(f"x_max{s}", [P, 1]) for s in range(NS)]
        x_seen = [sb(f"x_seen{s}", [P, 1]) for s in range(NS)]
        x_all = [sb(f"x_all{s}", [P, 1]) for s in range(NS)]
        bound = [sb(f"bound{s}", [P, NSC]) for s in range(NS)]
        power = [sb(f"power{s}", [P, NSC]) for s in range(NS)]
        scale = [sb(f"scale{s}", [P, NSC]) for s in range(NS)]
        factor = [sb(f"factor{s}", [P, 4]) for s in range(NS)]
        affine_next = [sb(f"affine_next{s}", [P, 4 + NBIAS]) for s in range(NS)]
        affine = [sb(f"affine{s}", [P, 4 + NBIAS]) for s in range(NS)]
        x_half = [sb(f"x_half{s}", [P, PH, 2, N], F16) for s in range(NS)]
        conv_in = [[sb(f"conv_in{l}_{s}", [P, G, 2, N + 2], F16) for s in range(NS)] for l in range(2)]
        conv_out = [sb(f"conv_out{s}", [P, G, 2, N], F16) for s in range(NS)]
        mix_in = [sb(f"mix_in{s}", [P, PH, 2, N], F16) for s in range(NS)]
        value = [sb(f"value{s}", [P, 4, N]) for s in range(NS)]
        y_out = [sb(f"y_out{s}", [P, L]) for s in range(NS)]
        expert_rows = [y_out[l][:, 0:NE * P].rearrange("p (k i) -> p k i", i=P) for l in range(2)]
        prod = [sb(f"prod{l}", [P, NE, P]) for l in range(2)]
        mat = [sb(f"mat{l}", [P, P]) for l in range(2)]
        mat_half = [[sb(f"mat_half{l}_{s}", [P, 2, P], F16) for s in range(NS)] for l in range(2)]
        banks = [ctx.enter_context(nc.psum_tensor(f"bank{i}", [P, N], F32)) for i in range(8)]

        load_rows = [(expert_rows[0], t["expert_rows0"]), (conv_rows[1][:], t["conv_rows1"]),
                     (expert_rows[1], t["expert_rows1"])]

        rows_loaded = sem("rows_loaded")
        toep_loaded = sem("toep_loaded")
        small_loaded = sem("small_loaded")
        more_rows_loaded = sem("more_rows_loaded")
        experts_loaded = [sem(f"experts_loaded{l}") for l in range(2)]
        toep1_loaded = sem("toep1_loaded")
        residual_added = sem("residual_added")
        scale_ready = sem("weight_scale_ready")
        toep_high_ready = sem("toep_high_ready")
        x_loaded = [sem(f"x_loaded{s}") for s in range(NS)]
        x_max_ready = sem("x_max_ready")
        x_all_ready = sem("x_all_ready")
        x_scale_ready = sem("x_scale_ready")
        x_high = sem("x_high")
        x_split = sem("x_split")
        x_moved = [sem(f"x_moved{s}") for s in range(NS)]
        conv_moved = [[sem(f"conv_moved{l}_{s}") for s in range(NS)] for l in range(2)]
        affine_ready = sem("affine_ready")
        product = [sem(f"product{k}") for k in range(4)]
        valued = [sem(f"valued{k}") for k in range(3)]
        split = [sem(f"split{k}") for k in range(3)]
        y_ready = sem("y_ready")
        y_stored = [sem(f"y_stored{s}") for s in range(NS)]
        mat_ready = [sem(f"mat_ready{l}") for l in range(2)]
        pool_step = sem("pool_step")
        dve_step = sem("dve_step")
        ones_ready = sem("ones_ready")
        borders_zero = sem("borders_zero")
        first_row_ready = sem("first_row_ready")
        first_row_reduced = sem("first_row_reduced")
        toep_ready = sem("toep_ready")
        stats_ready = sem("stats_ready")
        stats_reduced = sem("stats_reduced")
        att_all_ready = sem("att_all_ready")
        router_product = sem("router_product")
        router_hidden = sem("router_hidden")
        logit_ready = sem("logit_ready")
        exp_ready = sem("exp_ready")
        att_ready = sem("att_ready")
        att_t_ready = sem("att_t_ready")
        spread_product = sem("spread_product")
        conv_bias_product = sem("conv_bias_product")
        mix_bias_product = sem("mix_bias_product")

        def sample(i, s):
            return i * NS + s

        def repeats(i):
            return not isinstance(i, int) or i > 0

        def halves(k, s, half, q):
            return conv_in[1][s][:, q, half, 1:N + 1] if k == 1 else conv_out[s][:, q, half, :]

        block = ctx.enter_context(nc.Block())

        @block.sync
        def _(sp):
            def load_x(b, s):
                sp.dma_start(x_in[s][:], t["x"][bass.ds(b, 1), :, :].rearrange("b c l -> (b c) l")
                             ).then_inc(x_loaded[s], 16)

            def move_x(i, s):
                sp.wait_ge(x_split, sample(i, s) + 1)
                for g in range(G):
                    sp.dma_start(conv_in[0][s][:, g, :, 1:N + 1], x_half[s][CG * g:CG * (g + 1)]
                                 ).then_inc(x_moved[s], 16)

            def move_conv(l, i, s):
                for g in range(G):
                    sp.wait_ge(split[2 * l], G * sample(i, s) + g + 1)
                    sp.dma_start(mix_in[s][CG * g:CG * (g + 1)], conv_out[s][:, g]).then_inc(conv_moved[l][s], 16)

            def store(i, s):
                b = sample(i, s)
                sp.wait_ge(y_ready, PH * (b + 1))
                sp.dma_start(out[bass.ds(b, 1), :, :].rearrange("b c l -> (b c) l"), y_out[s][:]
                             ).then_inc(y_stored[s], 16)

            sp.dma_start(conv_rows[0][:], t["conv_rows0"]).then_inc(rows_loaded, 16)
            load_x(0, A)
            sp.dma_start(eye[:], t["eye"]).then_inc(toep_loaded, 16)
            sp.dma_start(toep[0][:], t["toep0"]).then_inc(toep_loaded, 16)
            sp.dma_start(small[:], t["small"]).then_inc(small_loaded, 16)
            load_x(1, B)
            move_x(0, A)
            for dst, src in load_rows:
                sp.dma_start(dst, src).then_inc(more_rows_loaded, 16)
            sp.dma_start(experts[0][:], t["experts0"]).then_inc(experts_loaded[0], 16)
            move_x(0, B)
            sp.dma_start(eye_phases[:], t["eye_phases"]).then_inc(toep1_loaded, 16)
            sp.dma_start(toep[1][:], t["toep1"]).then_inc(toep1_loaded, 16)
            sp.dma_start(experts[1][:], t["experts1"]).then_inc(experts_loaded[1], 16)

            def turn(i, last, load):
                move_conv(0, i, A)
                if repeats(i):
                    store(i - 1, B)
                else:
                    load_x(sample(1, A), A)
                move_conv(0, i, B)
                if not repeats(i):
                    load_x(sample(1, B), B)
                move_conv(1, i, A)
                if not last:
                    move_x(i + 1, A)
                    if load:
                        load_x(sample(i + 2, A), A)
                move_conv(1, i, B)
                if not last:
                    move_x(i + 1, B)
                    if load:
                        load_x(sample(i + 2, B), B)
                store(i, A)

            turn(0, False, True)
            turn(1, False, True)
            with sp.Fori(2, PAIRS - 2) as i:
                turn(i, False, True)
            turn(PAIRS - 2, False, False)
            turn(PAIRS - 1, True, False)
            store(PAIRS - 1, B)
            for s in range(NS):
                sp.wait_ge(y_stored[s], 16 * PAIRS)

        @block.gpsimd
        def _(pool):
            SUMS = 5

            def all_reduce(i, s):
                b = sample(i, s)
                pool.wait_ge(x_max_ready, b + 1)
                nc.gpsimd.tensor_tensor(x_seen[s][:], x_max[s][:], x_max[s][:], ALU.add)
                nc.gpsimd.partition_all_reduce(x_all[s][:], x_max[s][:], P, MAX).then_inc(x_all_ready, 1)

            def mix_matrix(l, i, s, place):
                b = sample(i, s)
                done = place * SUMS
                if s or repeats(i):
                    pool.wait_ge(mat_ready[l], b)
                weight = att_all[l][:, bass.ds(b, 1), :].rearrange("p b k -> p (b k)").unsqueeze(2).broadcast_to([P, NE, P])
                nc.gpsimd.tensor_tensor(prod[l][:], experts[l][:], weight, ALU.mult).then_inc(pool_step, 1)
                half, n = NE // 2, 1
                while half:
                    pool.wait_ge(pool_step, done + n)
                    nc.gpsimd.tensor_tensor(prod[l][:, 0:half, :], prod[l][:, 0:half, :],
                                            prod[l][:, half:2 * half, :], ALU.add).then_inc(pool_step, 1)
                    half, n = half // 2, n + 1
                if repeats(i):
                    pool.wait_ge(product[2 * l + 1], PH * (b - NS + 1))
                pool.wait_ge(pool_step, done + n)
                nc.gpsimd.tensor_tensor(mat_half[l][s][:, HI, :], prod[l][:, 0, :], eye_scaled[l][:], ALU.add)
                nc.gpsimd.tensor_tensor(mat[l][:], prod[l][:, 0, :], eye_scaled[l][:], ALU.add).then_inc(pool_step, 1)
                pool.wait_ge(pool_step, done + n + 1)
                nc.gpsimd.tensor_tensor(mat_half[l][s][:, LO, :], mat[l][:], mat_half[l][s][:, HI, :], ALU.subtract
                                        ).then_inc(mat_ready[l], 1)

            nc.gpsimd.memset(ones[:], 1.0).then_inc(ones_ready, 1)
            pool.wait_ge(first_row_ready, 1)
            nc.gpsimd.partition_all_reduce(first_row_all[:], first_row[:], P, MAX).then_inc(first_row_reduced, 1)
            all_reduce(0, A)
            all_reduce(0, B)
            pool.wait_ge(stats_ready, 1)
            nc.gpsimd.partition_all_reduce(stats_all[:], stats[:], P, MAX).then_inc(stats_reduced, 1)
            pool.wait_ge(att_all_ready, 1)
            pool.wait_ge(experts_loaded[0], 16)
            mix_matrix(0, 0, A, 0)
            mix_matrix(0, 0, B, 1)
            pool.wait_ge(experts_loaded[1], 16)
            mix_matrix(1, 0, A, 2)

            def turn(i):
                all_reduce(i, A)
                mix_matrix(1, i - 1, B, 4 * i - 1)
                mix_matrix(0, i, A, 4 * i)
                all_reduce(i, B)
                mix_matrix(0, i, B, 4 * i + 1)
                mix_matrix(1, i, A, 4 * i + 2)

            turn(1)
            with pool.Fori(2, PAIRS) as i:
                turn(i)
            mix_matrix(1, PAIRS - 1, B, 4 * PAIRS - 1)

        @block.scalar
        def _(act):
            def high_x(i, s):
                b = sample(i, s)
                act.wait_ge(x_scale_ready, b + 1)
                if repeats(i):
                    act.wait_ge(x_moved[s], 16 * MOVES * i)
                nc.scalar.activation(x_half[s][:, :, HI, :], x_in[s][:].rearrange("c (n p) -> c p n", p=PH),
                                     ACT.Identity, scale=scale[s][:, S_X:S_X + 1]).then_inc(x_high, 1)

            def evacuate(k, i, s, qs=range(4)):
                b = sample(i, s)
                for q in qs:
                    act.wait_ge(product[k], 4 * b + q + 1)
                    if k < 3:
                        dst, done = value[s][:, q, :], valued[k]
                    else:
                        dst, done = y_out[s][:].rearrange("c (n p) -> c p n", p=PH)[:, q, :], y_ready
                    col = 4 + bias_column(k, q)
                    nc.scalar.activation(dst, banks[4 * s + q][:], ACT.Identity, bias=affine[s][:, col:col + 1],
                                         scale=affine[s][:, k:k + 1]).then_inc(done, 1)

            high_x(0, 0)
            act.wait_ge(small_loaded, 16)
            for l in range(2):
                act.wait_ge(router_product, l + 1)
                nc.scalar.activation(hid[l][:, 0, :], banks[4 + l][:, 0:NB], ACT.Gelu, bias=b0[l]).then_inc(router_hidden, 1)
            for l in range(2):
                act.wait_ge(router_product, l + 3)
                nc.scalar.activation(hid[l][:, 1, :], banks[4 + l][:, NB:2 * NB], ACT.Gelu, bias=b1[l]).then_inc(router_hidden, 1)
            for l in range(2):
                act.wait_ge(logit_ready, l + 1)
                nc.scalar.activation(expo[l][:], logit[l][:], ACT.Exp, accum_out=total[l][:]).then_inc(exp_ready, 1)
            high_x(0, 1)

            def output(i, s):
                if repeats(i):
                    act.wait_ge(y_stored[s], 16 * i)
                evacuate(3, i, s)

            act.wait_ge(affine_ready, 1)
            evacuate(0, 0, A)
            act.wait_ge(affine_ready, 2)
            evacuate(0, 0, B, (0, 1))
            act.wait_ge(scale_ready, 1)
            act.wait_ge(residual_added, 1)
            nc.scalar.activation(toep_half[1][:, HI].rearrange("p g m c -> p (g m c)"),
                                 toep[1][:].rearrange("p g m c -> p (g m c)"), ACT.Identity,
                                 scale=weight_scale[:, 2:3]).then_inc(toep_high_ready, 1)
            evacuate(0, 0, B, (2, 3))
            evacuate(1, 0, A)
            evacuate(2, 0, A)
            evacuate(1, 0, B)
            high_x(1, A)
            evacuate(2, 0, B)
            output(0, A)
            high_x(1, B)

            def turn(i, last):
                act.wait_ge(affine_ready, sample(i, A) + 1)
                evacuate(0, i, A)
                output(i - 1, B)
                act.wait_ge(affine_ready, sample(i, B) + 1)
                if not last:
                    high_x(i + 1, A)
                evacuate(0, i, B)
                evacuate(1, i, A)
                evacuate(2, i, A)
                evacuate(1, i, B)
                if not last:
                    high_x(i + 1, B)
                evacuate(2, i, B)
                output(i, A)

            turn(1, False)
            with act.Fori(2, PAIRS - 1) as i:
                turn(i, False)
            turn(PAIRS - 1, True)
            output(PAIRS - 1, B)

        @block.vector
        def _(dve):
            before, made = [0], [0]
            PER_TURN = 3 * NS * 4 + NS * 2 + NS * 5

            def step(ins, turn=1):
                made[0] += 1
                ins.then_inc(dve_step, 1)
                dve.wait_ge(dve_step, before[0] + made[0] + PER_TURN * (turn - 1))

            def largest_x(i, s):
                dve.wait_ge(x_loaded[s], 16 * (i + 1))
                nc.vector.tensor_reduce(x_max[s][:], x_in[s][:], AX.X, ALU.max, apply_absolute_value=True
                                        ).then_inc(x_max_ready, 1)

            def scale_x(i, s, turn):
                dve.wait_ge(x_all_ready, sample(i, s) + 1)
                step(nc.vector.tensor_scalar(bound[s][:, S_X:S_X + 1], x_all[s][:], 1 / TOP, TINY, ALU.mult, ALU.max), turn)
                step(nc.vector.tensor_scalar(power[s][:, S_X:S_X + 1].bitcast(I32), bound[s][:, S_X:S_X + 1].bitcast(I32),
                                             EXPONENT, None, ALU.bitwise_and), turn)
                nc.vector.reciprocal(scale[s][:, S_X:S_X + 1], power[s][:, S_X:S_X + 1]).then_inc(x_scale_ready, 1)

            def low_x(i, s):
                dve.wait_ge(x_high, sample(i, s) + 1)
                nc.vector.scalar_tensor_tensor(x_half[s][:, :, LO, :], x_in[s][:].rearrange("c (n p) -> c p n", p=PH),
                                               scale[s][:, S_X:S_X + 1], x_half[s][:, :, HI, :], ALU.mult, ALU.subtract
                                               ).then_inc(x_split, 1)

            def scale_values(i, s, turn):
                b = sample(i, s)
                rest = slice(S_X + 1, NSC)
                step(nc.vector.scalar_tensor_tensor(bound[s][:, rest], grow[:, rest], bound[s][:, S_X:S_X + 1],
                                                    shift[:, rest], ALU.mult, ALU.add), turn)
                step(nc.vector.tensor_scalar(power[s][:, rest].bitcast(I32), bound[s][:, rest].bitcast(I32), EXPONENT,
                                             None, ALU.bitwise_and), turn)
                step(nc.vector.reciprocal(scale[s][:, rest], power[s][:, rest]), turn)
                step(nc.vector.tensor_tensor(factor[s][:], power[s][:, 0:4], weight_undo[:], ALU.mult), turn)
                nc.vector.tensor_tensor(affine_next[s][:, 0:4], scale[s][:, 1:5], factor[s][:], ALU.mult)
                step(nc.vector.tensor_tensor(affine_next[s][:, 4:4 + NBIAS], scale[s][:, rest],
                                             biases[:, bass.ds(b, 1), :].rearrange("p b c -> p (b c)"), ALU.mult), turn)

            def halve(k, i, s, turn, qs=range(4)):
                b = sample(i, s)
                for q in qs:
                    dve.wait_ge(valued[k], 4 * b + q + 1)
                    step(nc.vector.tensor_copy(halves(k, s, HI, q), value[s][:, q, :]), turn)
                    nc.vector.tensor_tensor(halves(k, s, LO, q), value[s][:, q, :],
                                            halves(k, s, HI, q), ALU.subtract).then_inc(split[k], 1)

            def halve_toep(l):
                high, low = (toep_half[l][:, h].rearrange("p g m c -> p (g m c)") for h in (HI, LO))
                whole = toep[l][:].rearrange("p g m c -> p (g m c)")
                by = weight_scale[:, 2 * l:2 * l + 1]
                if l == 0:
                    step(nc.vector.tensor_scalar(high, whole, by, None, ALU.mult))
                else:
                    dve.wait_ge(toep_high_ready, 1)
                nc.vector.scalar_tensor_tensor(low, whole, by, high, ALU.mult, ALU.subtract).then_inc(toep_ready, 1)

            def add_residual(l):
                for g in range(G):
                    own = toep[l][:, g, 1, :]
                    ins = nc.vector.tensor_tensor(own, own, (eye, eye_phases)[l][:], ALU.add)
                if l == 0:
                    step(ins)
                else:
                    ins.then_inc(residual_added, 1)

            for l in range(2):
                for s in range(NS):
                    nc.vector.memset(conv_in[l][s][:, :, :, 0:1], 0.0)
                    last = nc.vector.memset(conv_in[l][s][:, :, :, N + 1:N + 2], 0.0)
            last.then_inc(borders_zero, 1)
            dve.wait_ge(rows_loaded, 16)
            nc.vector.tensor_reduce(first_row[:], conv_rows[0][:], AX.X, ALU.add, apply_absolute_value=True
                                    ).then_inc(first_row_ready, 1)
            largest_x(0, 0)
            dve.wait_ge(first_row_reduced, 1)
            step(nc.vector.tensor_scalar(first_row_all[:], first_row_all[:], 1.0, None, ALU.add))
            step(nc.vector.tensor_scalar(weight_undo[:, 0:1], first_row_all[:], 1 / TOP, None, ALU.mult))
            step(nc.vector.tensor_scalar(weight_undo[:, 0:1].bitcast(I32), weight_undo[:, 0:1].bitcast(I32), EXPONENT,
                                         None, ALU.bitwise_and))
            step(nc.vector.reciprocal(weight_scale[:, 0:1], weight_undo[:, 0:1]))
            scale_x(0, 0, 1)
            dve.wait_ge(toep_loaded, 32)
            add_residual(0)
            low_x(0, 0)
            halve_toep(0)
            dve.wait_ge(small_loaded, 16)
            for l in range(2):
                dve.wait_ge(router_product, l + 5)
                step(nc.vector.tensor_tensor(logit[l][:], banks[4 + l][0:NB, 128:128 + NE], b2[l], ALU.add))
                step(nc.vector.tensor_reduce(top[l][:], logit[l][:], AX.X, ALU.max))
                nc.vector.tensor_scalar(logit[l][:], logit[l][:], top[l][:], None, ALU.subtract).then_inc(logit_ready, 1)
            largest_x(0, B)
            for l in range(2):
                dve.wait_ge(exp_ready, l + 1)
                step(nc.vector.reciprocal(total[l][:], total[l][:]))
                step(nc.vector.tensor_scalar(att[l][:], expo[l][:], total[l][:], None, ALU.mult))
                nc.vector.tensor_tensor(att_diag[l][:], eye[0:NB, 0:NB].unsqueeze(2).broadcast_to([NB, NB, NE]),
                                        att[l][:].unsqueeze(1).broadcast_to([NB, NB, NE]), ALU.mult).then_inc(att_ready, 1)
            scale_x(0, B, 1)
            dve.wait_ge(more_rows_loaded, 16 * len(load_rows))
            for l in range(2):
                ins = nc.vector.tensor_reduce(row_top[:, l, :], expert_rows[l], AX.X, ALU.add,
                                              apply_absolute_value=True)
            step(ins)
            low_x(0, B)
            for l in range(2):
                dve.wait_ge(spread_product, l + 1)
                nc.vector.tensor_copy(att_t[l][:], banks[4 + l][0:NE, 160:160 + NB]).then_inc(att_t_ready, 1)
            for l in range(2):
                nc.vector.tensor_reduce(stats[:, 2 * l:2 * l + 1], row_top[:, l, :], AX.X, ALU.max)
            nc.vector.tensor_reduce(stats[:, 1:2], conv_rows[1][:], AX.X, ALU.add, apply_absolute_value=True)
            dve.wait_ge(conv_bias_product, 1)
            by_column = biases[:].rearrange("p b n -> p n b")

            def keep_biases(k, groups):
                nc.vector.tensor_copy(by_column[:, k:k + 1, :], groups[:, 0:1, :])
                more = S_MORE[k + 1] - 1
                return nc.vector.tensor_copy(by_column[:, more:more + G - 1, :], groups[:, 1:G, :])

            for l in range(2):
                ins = nc.vector.tensor_tensor(conv_bias[l][:], banks[6][:, G * NB * l:G * NB * (l + 1)].rearrange(
                    "p (g b) -> p g b", g=G), fside.unsqueeze(2).broadcast_to([P, G, NB]), ALU.add)
            step(ins)
            for l in range(2):
                nc.vector.tensor_reduce(stats[:, 3 + 2 * l:4 + 2 * l], conv_bias[l][:].rearrange("p g b -> p (g b)"), AX.X,
                                        ALU.max, apply_absolute_value=True)
            dve.wait_ge(mix_bias_product, 1)
            nc.vector.tensor_reduce(stats[:, 4:5], banks[7][:, 0:G * NB], AX.X, ALU.max, apply_absolute_value=True
                                    ).then_inc(stats_ready, 1)
            for l in range(2):
                keep_biases(2 * l, conv_bias[l][:])
            keep_biases(1, banks[7][:, 0:G * NB].rearrange("p (g b) -> p g b", g=G))
            step(nc.vector.tensor_copy(biases[:, :, 3], banks[7][:, G * NB:(G + 1) * NB]))
            dve.wait_ge(stats_reduced, 1)
            nc.vector.tensor_scalar(stats_all[:, 3:6], stats_all[:, 3:6], 1 / TOP, None, ALU.mult)
            step(nc.vector.tensor_scalar(stats_all[:, 0:3], stats_all[:, 0:3], 1.0, None, ALU.add))
            step(nc.vector.tensor_scalar(weight_undo[:, 1:4], stats_all[:, 0:3], 1 / TOP, None, ALU.mult))
            step(nc.vector.tensor_scalar(weight_undo[:, 1:4].bitcast(I32), weight_undo[:, 1:4].bitcast(I32), EXPONENT,
                                         None, ALU.bitwise_and))
            step(nc.vector.reciprocal(weight_scale[:, 1:4], weight_undo[:, 1:4]))
            nc.vector.drain().then_inc(scale_ready, 1)
            for l in range(2):
                by = weight_scale[:, 2 * l + 1:2 * l + 2]
                nc.vector.tensor_scalar(eye_scaled[l][:], eye[:], by, None, ALU.mult)
                last = nc.vector.tensor_scalar(att_all[l][:], banks[4 + l][:, 256:512].rearrange("p (b k) -> p b k", k=NE),
                                               by, None, ALU.mult)
            last.then_inc(att_all_ready, 1)
            row0, row1, row2 = first_row_all[:], stats_all[:, 0:1], stats_all[:, 1:2]
            nc.vector.memset(grow[:, S_OUT:S_OUT + 1], 0.0)
            nc.vector.memset(shift[:, S_OUT:S_OUT + 1], 1.0)
            nc.vector.tensor_copy(grow[:, S_MIX0:S_MIX0 + 1], row0)
            nc.vector.tensor_copy(shift[:, S_MIX0:S_MIX0 + 1], stats_all[:, 3:4])
            nc.vector.tensor_tensor(grow[:, S_CONV1:S_CONV1 + 1], row0, row1, ALU.mult)
            step(nc.vector.tensor_scalar(shift[:, S_CONV1:S_CONV1 + 1], stats_all[:, 3:4], row1, stats_all[:, 4:5],
                                         ALU.mult, ALU.add))
            nc.vector.tensor_tensor(grow[:, S_MIX1:S_MIX1 + 1], grow[:, S_CONV1:S_CONV1 + 1], row2, ALU.mult)
            nc.vector.tensor_scalar(shift[:, S_MIX1:S_MIX1 + 1], shift[:, S_CONV1:S_CONV1 + 1], row2, stats_all[:, 5:6],
                                    ALU.mult, ALU.add)
            step(nc.vector.drain())
            for a in (grow, shift):
                for of, at in S_MORE.items():
                    last = nc.vector.tensor_copy(a[:, at:at + G - 1], a[:, of:of + 1].broadcast_to([P, G - 1]))
            step(last)

            def next_affine(i, s):
                if repeats(i):
                    dve.wait_ge(y_ready, PH * (sample(i, s) - 1))
                nc.vector.tensor_copy(affine[s][:], affine_next[s][:]).then_inc(affine_ready, 1)

            scale_values(0, A, 1)
            next_affine(0, A)
            halve(0, 0, A, 1)
            scale_values(0, B, 1)
            next_affine(0, B)
            dve.wait_ge(toep1_loaded, 32)
            add_residual(1)
            halve(0, 0, B, 1, (0, 1))
            halve_toep(1)
            halve(0, 0, B, 1, (2, 3))
            halve(1, 0, A, 1)
            largest_x(1, A)
            halve(2, 0, A, 1, (0,))
            scale_x(1, A, 1)
            halve(2, 0, A, 1, (1, 2, 3))
            halve(1, 0, B, 1)
            low_x(1, A)
            scale_values(1, A, 1)
            halve(2, 0, B, 1, (0,))
            largest_x(1, B)
            halve(2, 0, B, 1, (1,))
            scale_x(1, B, 1)
            halve(2, 0, B, 1, (2, 3))
            low_x(1, B)
            before[0], made[0] = made[0], 0

            def turn(i, last):
                made[0] = 0
                next_affine(i, A)
                scale_values(i, B, i)
                halve(0, i, A, i, (0, 1))
                if not last:
                    largest_x(i + 1, A)
                halve(0, i, A, i, (2, 3))
                if not last:
                    scale_x(i + 1, A, i)
                next_affine(i, B)
                if not last:
                    low_x(i + 1, A)
                halve(0, i, B, i)
                halve(1, i, A, i)
                halve(2, i, A, i, (0,))
                if not last:
                    largest_x(i + 1, B)
                halve(2, i, A, i, (1, 2))
                if not last:
                    scale_x(i + 1, B, i)
                halve(2, i, A, i, (3,))
                halve(1, i, B, i)
                if not last:
                    low_x(i + 1, B)
                halve(2, i, B, i)
                if not last:
                    scale_values(i + 1, A, i)
                    assert made[0] == PER_TURN

            turn(1, False)
            with dve.Fori(2, PAIRS - 1) as i:
                turn(i, False)
            turn(PAIRS - 1, True)

        @block.tensor
        def _(pe):
            def conv(l, i, s, gs=range(G)):
                b = sample(i, s)
                if l == 0:
                    pe.wait_ge(x_moved[s], 16 * MOVES * (i + 1))
                for g in gs:
                    if l == 0 and repeats(i):
                        pe.wait_ge(y_ready, 4 * (b - NS) + g + 1)
                    if l == 1:
                        pe.wait_ge(split[1], G * b + g + 1)
                    n = 0
                    for m in range(REACH):
                        for w, x in PASSES:
                            last = nc.tensor.matmul(banks[4 * s + g][:], toep_half[l][:, w, g, m, :],
                                                    conv_in[l][s][:, g, x, m:m + N], start=n == 0,
                                                    stop=n == REACH * len(PASSES) - 1)
                            n += 1
                    last.then_inc(product[2 * l], 1)

            def mix(l, i, s):
                b = sample(i, s)
                pe.wait_ge(mat_ready[l], b + 1)
                pe.wait_ge(conv_moved[l][s], 16 * MOVES * (i + 1))
                for h in range(G):
                    bank = banks[4 * s + h]
                    for n, (w, x) in enumerate(PASSES):
                        flags = dict(start=n == 0, stop=n == len(PASSES) - 1)
                        if l == 0:
                            for p in range(PH):
                                last = nc.tensor.matmul(bank[CG * p:CG * (p + 1), :],
                                                        mat_half[0][s][:, w, CG * h:CG * (h + 1)],
                                                        mix_in[s][:, p, x, :], tile_position=(0, CG * p), **flags)
                        else:
                            last = nc.tensor.matmul(bank[:], mat_half[1][s][:, w, :], mix_in[s][:, h, x, :], **flags)
                    last.then_inc(product[2 * l + 1], 1)

            pe.wait_ge(small_loaded, 16)
            for l in range(2):
                nc.tensor.matmul(banks[4 + l][:, 0:NB], w0[l], cond_t, start=True, stop=True).then_inc(router_product, 1)
            for l in range(2):
                for g in range(G):
                    last = nc.tensor.matmul(banks[6][:, NB * (G * l + g):NB * (G * l + g + 1)],
                                            cw_t[l][:, P * g:P * (g + 1)], cond_t, start=True, stop=True)
            last.then_inc(conv_bias_product, 1)
            for l in range(2):
                pe.wait_ge(router_hidden, l + 1)
                nc.tensor.matmul(banks[4 + l][:, NB:2 * NB], w1[l], hid[l][:, 0, :], start=True, stop=True
                                 ).then_inc(router_product, 1)
            for l in range(2):
                pe.wait_ge(router_hidden, l + 3)
                nc.tensor.matmul(banks[4 + l][0:NB, 128:128 + NE], hid[l][:, 1, :], w2[l], start=True, stop=True
                                 ).then_inc(router_product, 1)
            pe.wait_ge(borders_zero, 1)
            pe.wait_ge(toep_ready, 1)
            conv(0, 0, A, (0,))
            pe.wait_ge(toep_loaded, 32)
            pe.wait_ge(ones_ready, 1)
            for l in range(2):
                pe.wait_ge(att_ready, l + 1)
                nc.tensor.matmul(banks[4 + l][0:NE, 160:160 + NB], att[l][:], eye[0:NB, 0:NB], start=True, stop=True)
                nc.tensor.matmul(banks[4 + l][:, 256:512], ones[:], att_diag[l][:].rearrange("p b k -> p (b k)"),
                                 start=True, stop=True).then_inc(spread_product, 1)
            conv(0, 0, A, (1,))
            pe.wait_ge(att_t_ready, 2)
            for h in range(G):
                for p in range(PH):
                    nc.tensor.matmul(banks[7][CG * p:CG * (p + 1), NB * h:NB * (h + 1)],
                                     bias_k[0][:, CG * h:CG * (h + 1)], att_t[0][:], start=True, stop=True,
                                     tile_position=(0, CG * p))
            nc.tensor.matmul(banks[7][:, G * NB:(G + 1) * NB], bias_k[1], att_t[1][:], start=True, stop=True
                             ).then_inc(mix_bias_product, 1)
            conv(0, 0, A, (2, 3))
            pe.wait_ge(att_all_ready, 1)
            conv(0, 0, B)
            mix(0, 0, A)
            pe.wait_ge(toep_ready, 2)
            conv(1, 0, A)
            mix(0, 0, B)
            conv(1, 0, B)
            mix(1, 0, A)

            def turn(i):
                conv(0, i, A)
                mix(1, i - 1, B)
                conv(0, i, B)
                mix(0, i, A)
                conv(1, i, A)
                mix(0, i, B)
                conv(1, i, B)
                mix(1, i, A)

            turn(1)
            with pe.Fori(2, PAIRS) as i:
                turn(i)
            mix(1, PAIRS - 1, B)


def toeplitz(w, phase_first):
    import numpy as np
    t = np.zeros((PH, CG, G, REACH, CG, PH), w.dtype)
    by_group = w.reshape(G, CG, CG, K)
    for p in range(PH):
        for q in range(PH):
            for m in range(REACH):
                tap = PH * (m - 1) + p - q + K // 2
                if 0 <= tap < K:
                    t[p, :, :, m, :, q] = by_group[:, :, :, tap].transpose(2, 0, 1)
    if not phase_first:
        t = t.swapaxes(0, 1)
    return t.reshape(P, G, REACH, P)


def phase_rows(a):
    import numpy as np
    by_i = a.reshape(G, CG, *a.shape[1:]).swapaxes(0, 1)
    return np.repeat(by_i, PH, axis=0)


def kernel(**inputs):
    import numpy as np
    import concourse.bacc as bacc
    from concourse.bass_utils import run_bass_kernel_spmd

    a = {k: np.asarray(v) for k, v in inputs.items()}
    eye = np.eye(P, dtype=np.float32)
    lay = {"x": a["x"], "eye": eye,
           "eye_phases": eye.reshape(P, CG, PH).swapaxes(1, 2).reshape(P, P).T}
    small = {"cond_t0": a["cond_128"].T, "fside0": phase_rows(a["fside_S_0"].reshape(P))}
    for l in range(2):
        conv, mix = f"L{2 * l}_cond_", f"L{2 * l + 1}_cond_"
        lay[f"toep{l}"] = toeplitz(a[conv + "weight"], phase_first=l == 1)
        lay[f"conv_rows{l}"] = a[conv + "weight"].reshape(P, CG * K)
        lay[f"experts{l}"] = a[mix + "weight"][..., 0].transpose(2, 0, 1)
        lay[f"expert_rows{l}"] = a[mix + "weight"][..., 0].transpose(1, 0, 2)
        small[f"cw_t{l}"] = phase_rows(a[conv + "c_weight"]).transpose(2, 1, 0).reshape(P, G * P)
        small[f"w0_{l}"], small[f"w1_{l}"], small[f"w2_{l}"] = a[mix + "W0"], a[mix + "W1"], a[mix + "W2"]
        small[f"b0_{l}"], small[f"b1_{l}"] = a[mix + "b0"].reshape(P, 1), a[mix + "b1"].reshape(P, 1)
        small[f"b2_{l}"] = np.broadcast_to(a[mix + "b2"], (NB, NE))
        small[f"bias_k{l}"] = a[mix + "bias_k"]
    lay["small"] = np.zeros((P, SMALL_COLUMNS), np.float32)
    for name, (rows, columns, at) in SMALL.items():
        lay["small"][:rows, at:at + columns] = small[name]
    lay = {k: np.ascontiguousarray(v) for k, v in lay.items()}
    nc = bacc.Bacc("TRN2", target_bir_lowering=False, num_devices=1)
    t = {k: nc.dram_tensor(f"in_{k}", v.shape, mybir.dt.from_np(v.dtype), kind="ExternalInput").ap()
         for k, v in lay.items()}
    out = nc.dram_tensor("out", (NB, P, L), F32, kind="ExternalOutput").ap()
    build(nc, t, out)
    r = run_bass_kernel_spmd(nc, [{f"in_{k}": v for k, v in lay.items()}], core_ids=[0])
    return r.results[0]["out"]
```
